# Optimizing a Trainium2 kernel written in Bass

```python
import numpy as np
import jax
import jax.numpy as jnp

def _softmax(x, axis=-1):
    return jax.nn.softmax(x, axis=axis)

def _gelu(x):
    return jax.nn.gelu(x, approximate=True)

def _silu(x):
    return jax.nn.silu(x)

def _sigmoid(x):
    return jax.nn.sigmoid(x)

def _layernorm(x, axis=-1, eps=1e-05):
    m = jnp.mean(x, axis=axis, keepdims=True)
    v = jnp.var(x, axis=axis, keepdims=True)
    return (x - m) / jnp.sqrt(v + eps)

def _scatter_add(tgt, idx, src, axis=0):
    return tgt.at[idx].add(src)

def _segment_sum(src, seg, n):
    return jax.ops.segment_sum(src, seg, n)
kernel_name = 'mk_prb_d2_jaxref_r8_b26417'

def setup_inputs(seed: int=0):
    np.random.seed(seed)
    _w = jnp.asarray

    def _L0_attn_setup():
        import jax, jax.numpy as jnp
        import numpy as np
        D_MODEL = 256
        N_QUERY = 4
        N_HEAD = 8
        D_HEAD = D_MODEL // (N_QUERY * N_HEAD)
        D_KV = D_HEAD * N_HEAD
        BATCH, SEQ = (2, 256)
        key = jax.random.key(seed)
        ks = jax.random.split(key, 5)
        w_scale = 1.0 / np.sqrt(D_MODEL).astype(np.float32)
        x = jax.random.normal(ks[0], (BATCH, SEQ, D_MODEL), jnp.float32)
        Wq = jax.random.normal(ks[1], (D_MODEL, D_MODEL), jnp.float32) * w_scale
        Wk = jax.random.normal(ks[2], (D_KV, D_MODEL), jnp.float32) * w_scale
        Wv = jax.random.normal(ks[3], (D_KV, D_MODEL), jnp.float32) * w_scale
        memory = jax.random.normal(ks[4], (D_KV, D_KV), jnp.float32) * 0.02
        memory_norm = jnp.ones((D_KV, 1), jnp.float32)
        memory_weight = jnp.ones((1,), jnp.float32)
        return dict(x=x, Wq=Wq, Wk=Wk, Wv=Wv, memory=memory, memory_norm=memory_norm, memory_weight=memory_weight)
    _L0_attn_in = _L0_attn_setup()

    def _L0_ffn_setup():
        import jax, jax.numpy as jnp
        import numpy as np
        BLOCK_SIZE = 32
        HIDDEN_SIZE = 256
        MLP_DIM = 2048
        NVFP4_LUT = jnp.array([0.0, 0.5, 1.0, 1.5, 2.0, 3.0, 4.0, 6.0, 0.0, -0.5, -1.0, -1.5, -2.0, -3.0, -4.0, -6.0], dtype=jnp.float32)

        def dequant_nvfp4(W_packed, scales, block=BLOCK_SIZE):
            N = W_packed.shape[0]
            low = W_packed & 15
            high = W_packed >> 4 & 15
            idx = jnp.stack([low, high], axis=-1).reshape(N, -1)
            vals = NVFP4_LUT[idx]
            K = vals.shape[1]
            vals = vals.reshape(N, K // block, block) * scales[:, :, None]
            return vals.reshape(N, K)
        key = jax.random.key(seed)
        ks = jax.random.split(key, 7)
        x = jax.random.normal(ks[0], (4, 32, HIDDEN_SIZE), dtype=jnp.float32)
        gate_W_packed = jax.random.randint(ks[1], (MLP_DIM, HIDDEN_SIZE // 2), 0, 32, dtype=jnp.int32)
        gate_scales = jax.random.uniform(ks[2], (MLP_DIM, HIDDEN_SIZE // BLOCK_SIZE), dtype=jnp.float32) * 0.1 + 0.001
        up_W_packed = jax.random.randint(ks[3], (MLP_DIM, HIDDEN_SIZE // 2), 0, 32, dtype=jnp.int32)
        up_scales = jax.random.uniform(ks[4], (MLP_DIM, HIDDEN_SIZE // BLOCK_SIZE), dtype=jnp.float32) * 0.1 + 0.001
        down_W_packed = jax.random.randint(ks[5], (HIDDEN_SIZE, MLP_DIM // 2), 0, 32, dtype=jnp.int32)
        down_scales = jax.random.uniform(ks[6], (HIDDEN_SIZE, MLP_DIM // BLOCK_SIZE), dtype=jnp.float32) * 0.1 + 0.001
        return {'x': x, 'gate_W_packed': gate_W_packed, 'gate_scales': gate_scales, 'up_W_packed': up_W_packed, 'up_scales': up_scales, 'down_W_packed': down_W_packed, 'down_scales': down_scales}
    _L0_ffn_in = _L0_ffn_setup()

    def _L1_attn_setup():
        import jax, jax.numpy as jnp
        import numpy as np
        import math
        B, T, C, H, K = (2, 512, 256, 16, 4)
        D = C // H

        def _ln(t, g, b, eps=1e-05):
            m = t.mean(-1, keepdims=True)
            v = t.var(-1, keepdims=True)
            return (t - m) / jnp.sqrt(v + eps) * g + b

        def _l2n(t, eps=1e-12):
            return t / jnp.maximum(jnp.linalg.norm(t, axis=-1, keepdims=True), eps)
        key = jax.random.key(seed)
        ks = jax.random.split(key, 16)
        s = 0.02
        target = 1.0 - np.exp(np.linspace(math.log(1 - 0.9), math.log(1 - 0.999), H))
        gamma_b = jnp.asarray(np.log(target / (1 - target)), dtype=jnp.float32)
        inp = {'x': jax.random.normal(ks[0], (B, T, C), jnp.float32), 'Wq': jax.random.normal(ks[1], (C, C), jnp.float32) * s, 'Wk': jax.random.normal(ks[2], (C, C), jnp.float32) * s, 'Wv': jax.random.normal(ks[3], (C, C), jnp.float32) * s, 'Wo': jax.random.normal(ks[4], (C, C), jnp.float32) * s, 'conv_w': jax.random.normal(ks[5], (C, 1, K), jnp.float32) * s, 'conv_b': jnp.zeros((C,), jnp.float32), 'ig_w': jax.random.normal(ks[6], (C, C), jnp.float32) * s, 'ig_b': jnp.full((C,), -3.0, jnp.float32), 'og_w': jax.random.normal(ks[7], (C, C), jnp.float32) * s, 'og_b': jnp.zeros((C,), jnp.float32), 'gamma_w': jax.random.normal(ks[8], (H, C), jnp.float32) * (s * 0.1), 'gamma_b': gamma_b, 'vn_g': jnp.ones((D,), jnp.float32), 'vn_b': jnp.zeros((D,), jnp.float32), 'gn_g': jnp.ones((C,), jnp.float32), 'gn_b': jnp.zeros((C,), jnp.float32), 'mn_g': jnp.ones((D,), jnp.float32), 'mn_b': jnp.zeros((D,), jnp.float32)}
        return inp
    _L1_attn_in = _L1_attn_setup()

    def _L1_ffn_setup():
        import jax, jax.numpy as jnp
        import numpy as np
        EPS = 1e-08

        def _quantize(w):
            gamma = jnp.mean(jnp.abs(w))
            return jnp.clip(jnp.round(w / (gamma + EPS)), -1.0, 1.0)

        def _bitlinear(x, w):
            return jnp.matmul(x, _quantize(w).T)
        key = jax.random.key(seed)
        k1, k2, k3, k4 = jax.random.split(key, 4)
        d, h = (256, 704)
        x = jax.random.normal(k1, (4, 256, d), dtype=jnp.float32)
        w1 = jax.random.normal(k2, (h, d), dtype=jnp.float32)
        w2 = jax.random.normal(k3, (h, d), dtype=jnp.float32)
        w3 = jax.random.normal(k4, (d, h), dtype=jnp.float32)
        return {'x': x, 'w1': w1, 'w2': w2, 'w3': w3}
    _L1_ffn_in = _L1_ffn_setup()
    _d = {'L0_attn_x': _L0_attn_in['x'], 'L0_attn_Wq': _L0_attn_in['Wq'], 'L0_attn_Wk': _L0_attn_in['Wk'], 'L0_attn_Wv': _L0_attn_in['Wv'], 'L0_attn_memory': _L0_attn_in['memory'], 'L0_attn_memory_norm': _L0_attn_in['memory_norm'], 'L0_attn_memory_weight': _L0_attn_in['memory_weight'], 'L0_ffn_gate_W_packed': _L0_ffn_in['gate_W_packed'], 'L0_ffn_gate_scales': _L0_ffn_in['gate_scales'], 'L0_ffn_up_W_packed': _L0_ffn_in['up_W_packed'], 'L0_ffn_up_scales': _L0_ffn_in['up_scales'], 'L0_ffn_down_W_packed': _L0_ffn_in['down_W_packed'], 'L0_ffn_down_scales': _L0_ffn_in['down_scales'], 'L1_attn_Wq': _L1_attn_in['Wq'], 'L1_attn_Wk': _L1_attn_in['Wk'], 'L1_attn_Wv': _L1_attn_in['Wv'], 'L1_attn_Wo': _L1_attn_in['Wo'], 'L1_attn_conv_w': _L1_attn_in['conv_w'], 'L1_attn_conv_b': _L1_attn_in['conv_b'], 'L1_attn_ig_w': _L1_attn_in['ig_w'], 'L1_attn_ig_b': _L1_attn_in['ig_b'], 'L1_attn_og_w': _L1_attn_in['og_w'], 'L1_attn_og_b': _L1_attn_in['og_b'], 'L1_attn_gamma_w': _L1_attn_in['gamma_w'], 'L1_attn_gamma_b': _L1_attn_in['gamma_b'], 'L1_attn_vn_g': _L1_attn_in['vn_g'], 'L1_attn_vn_b': _L1_attn_in['vn_b'], 'L1_attn_gn_g': _L1_attn_in['gn_g'], 'L1_attn_gn_b': _L1_attn_in['gn_b'], 'L1_attn_mn_g': _L1_attn_in['mn_g'], 'L1_attn_mn_b': _L1_attn_in['mn_b'], 'L1_ffn_w1': _L1_ffn_in['w1'], 'L1_ffn_w2': _L1_ffn_in['w2'], 'L1_ffn_w3': _L1_ffn_in['w3']}
    _x0 = _d['L0_attn_x']
    _d['L0_attn_x'] = jax.random.normal(jax.random.fold_in(jax.random.key(seed), 1), (8, 256, 256), dtype=_x0.dtype)
    del _x0
    return _d

def reference(L0_attn_x, L0_attn_Wq, L0_attn_Wk, L0_attn_Wv, L0_attn_memory, L0_attn_memory_norm, L0_attn_memory_weight, L0_ffn_gate_W_packed, L0_ffn_gate_scales, L0_ffn_up_W_packed, L0_ffn_up_scales, L0_ffn_down_W_packed, L0_ffn_down_scales, L1_attn_Wq, L1_attn_Wk, L1_attn_Wv, L1_attn_Wo, L1_attn_conv_w, L1_attn_conv_b, L1_attn_ig_w, L1_attn_ig_b, L1_attn_og_w, L1_attn_og_b, L1_attn_gamma_w, L1_attn_gamma_b, L1_attn_vn_g, L1_attn_vn_b, L1_attn_gn_g, L1_attn_gn_b, L1_attn_mn_g, L1_attn_mn_b, L1_ffn_w1, L1_ffn_w2, L1_ffn_w3):

    def _L0_attn_ref(x, Wq, Wk, Wv, memory, memory_norm, memory_weight):
        import jax, jax.numpy as jnp
        import numpy as np
        D_MODEL = 256
        N_QUERY = 4
        N_HEAD = 8
        D_HEAD = D_MODEL // (N_QUERY * N_HEAD)
        D_KV = D_HEAD * N_HEAD
        BATCH, SEQ = (2, 256)
        b, s, d = x.shape
        q = x @ Wq.T
        k = x @ Wk.T
        v = x @ Wv.T
        qh = q.reshape(b, s, N_QUERY, N_HEAD, D_HEAD)
        kh = k.reshape(b, s, N_HEAD, D_HEAD)
        vh = v.reshape(b, s, N_HEAD, D_HEAD)
        scale = np.float32(1.0 / np.sqrt(np.float32(D_HEAD)))
        scores = jnp.einsum('bsqhd,bthd->bqhst', qh, kh) * scale
        probs = jax.nn.softmax(scores, axis=-1)
        a_dot = jnp.einsum('bqhst,bthd->bsqhd', probs, vh)
        a_dot = a_dot.reshape(b, s, N_QUERY * N_HEAD, D_HEAD)
        sigma_q = jax.nn.elu(q.reshape(b, s, N_QUERY, D_KV))
        a_mem = sigma_q @ memory / (sigma_q @ memory_norm)
        a_mem = a_mem.reshape(b, s, N_QUERY * N_HEAD, D_HEAD)
        w = jax.nn.sigmoid(memory_weight)
        out = a_dot * (1.0 - w) + a_mem * w
        return out.reshape(b, s, D_MODEL)

    def _L0_ffn_ref(x, gate_W_packed, gate_scales, up_W_packed, up_scales, down_W_packed, down_scales):
        import jax, jax.numpy as jnp
        import numpy as np
        BLOCK_SIZE = 32
        HIDDEN_SIZE = 256
        MLP_DIM = 2048
        NVFP4_LUT = jnp.array([0.0, 0.5, 1.0, 1.5, 2.0, 3.0, 4.0, 6.0, 0.0, -0.5, -1.0, -1.5, -2.0, -3.0, -4.0, -6.0], dtype=jnp.float32)

        def dequant_nvfp4(W_packed, scales, block=BLOCK_SIZE):
            N = W_packed.shape[0]
            low = W_packed & 15
            high = W_packed >> 4 & 15
            idx = jnp.stack([low, high], axis=-1).reshape(N, -1)
            vals = NVFP4_LUT[idx]
            K = vals.shape[1]
            vals = vals.reshape(N, K // block, block) * scales[:, :, None]
            return vals.reshape(N, K)
        B, S, H = x.shape
        xt = x.reshape(B * S, H)
        Wg = dequant_nvfp4(gate_W_packed, gate_scales)
        Wu = dequant_nvfp4(up_W_packed, up_scales)
        Wd = dequant_nvfp4(down_W_packed, down_scales)
        gate = jnp.einsum('th,nh->tn', xt, Wg)
        up = jnp.einsum('th,nh->tn', xt, Wu)
        gelu = jnp.tanh(0.7978845608028654 * (gate + 0.044715 * gate ** 3)) * gate * 0.5 + gate * 0.5
        inter = gelu * up
        out = jnp.einsum('tn,hn->th', inter, Wd)
        return out.reshape(B, S, H)

    def _L1_attn_ref(x, Wq, Wk, Wv, Wo, conv_w, conv_b, ig_w, ig_b, og_w, og_b, gamma_w, gamma_b, vn_g, vn_b, gn_g, gn_b, mn_g, mn_b):
        import jax, jax.numpy as jnp
        import numpy as np
        import math
        B, T, C, H, K = (2, 512, 256, 16, 4)
        D = C // H

        def _ln(t, g, b, eps=1e-05):
            m = t.mean(-1, keepdims=True)
            v = t.var(-1, keepdims=True)
            return (t - m) / jnp.sqrt(v + eps) * g + b

        def _l2n(t, eps=1e-12):
            return t / jnp.maximum(jnp.linalg.norm(t, axis=-1, keepdims=True), eps)
        Bs, Ts, Cs = x.shape
        Hs = gamma_w.shape[0]
        Ds = Cs // Hs
        Ks = conv_w.shape[-1]
        xt = jnp.transpose(x, (0, 2, 1))
        xc = jax.lax.conv_general_dilated(xt, conv_w, window_strides=(1,), padding=[(Ks - 1, 0)], dimension_numbers=('NCH', 'OIH', 'NCH'), feature_group_count=Cs)
        xc = jax.nn.silu(jnp.transpose(xc + conv_b[None, :, None], (0, 2, 1)))
        q = _l2n((x @ Wq.T).reshape(Bs, Ts, Hs, Ds))
        k = _l2n((x @ Wk.T).reshape(Bs, Ts, Hs, Ds))
        v = _ln((x @ Wv.T).reshape(Bs, Ts, Hs, Ds), vn_g, vn_b)
        i_gate = jax.nn.sigmoid(xc @ ig_w.T + ig_b).reshape(Bs, Ts, Hs, Ds)
        gamma = jax.nn.sigmoid(xc @ gamma_w.T + gamma_b)[..., None]
        a = jnp.broadcast_to(gamma, (Bs, Ts, Hs, Ds))
        b = i_gate * k * v

        def comb(left, right):
            aL, bL = left
            aR, bR = right
            return (aL * aR, bL * aR + bR)
        _, mem = jax.lax.associative_scan(comb, (a, b), axis=1)
        out = _ln(mem, mn_g, mn_b) * q
        o = out.reshape(Bs * Ts, Hs, Ds)
        m = o.mean(-1, keepdims=True)
        var = o.var(-1, keepdims=True)
        o = (o - m) / jnp.sqrt(var + 1e-05)
        o = o.reshape(Bs * Ts, Cs) * gn_g + gn_b
        o = o.reshape(Bs, Ts, Cs)
        o = o * jax.nn.sigmoid(xc @ og_w.T + og_b)
        return o @ Wo.T

    def _L1_ffn_ref(x, w1, w2, w3):
        import jax, jax.numpy as jnp
        import numpy as np
        EPS = 1e-08

        def _quantize(w):
            gamma = jnp.mean(jnp.abs(w))
            return jnp.clip(jnp.round(w / (gamma + EPS)), -1.0, 1.0)

        def _bitlinear(x, w):
            return jnp.matmul(x, _quantize(w).T)
        x1 = _bitlinear(x, w1)
        x2 = _bitlinear(x, w2)
        hidden = jax.nn.sigmoid(x1) * x2
        return _bitlinear(hidden, w3)
    x = L0_attn_x
    xn = _layernorm(x, axis=-1)
    x = x + _L0_attn_ref(xn, L0_attn_Wq, L0_attn_Wk, L0_attn_Wv, L0_attn_memory, L0_attn_memory_norm, L0_attn_memory_weight) + _L0_ffn_ref(xn, L0_ffn_gate_W_packed, L0_ffn_gate_scales, L0_ffn_up_W_packed, L0_ffn_up_scales, L0_ffn_down_W_packed, L0_ffn_down_scales)
    xn = _layernorm(x, axis=-1)
    x = x + _L1_attn_ref(xn, L1_attn_Wq, L1_attn_Wk, L1_attn_Wv, L1_attn_Wo, L1_attn_conv_w, L1_attn_conv_b, L1_attn_ig_w, L1_attn_ig_b, L1_attn_og_w, L1_attn_og_b, L1_attn_gamma_w, L1_attn_gamma_b, L1_attn_vn_g, L1_attn_vn_b, L1_attn_gn_g, L1_attn_gn_b, L1_attn_mn_g, L1_attn_mn_b) + _L1_ffn_ref(xn, L1_ffn_w1, L1_ffn_w2, L1_ffn_w3)
    return x

_drawn_inputs = setup_inputs


def setup_inputs(seed=0):
    import zlib

    import numpy as np

    out = dict(_drawn_inputs(seed))
    spreads = {'L0_attn_memory_norm': (1.0, 0.2),
     'L1_attn_conv_b': (0.0, 2.0),
     'L1_attn_ig_b': (-3.0, 0.6),
     'L1_attn_og_b': (0.0, 2.0),
     'L1_attn_vn_g': (1.0, 0.6),
     'L1_attn_vn_b': (0.0, 2.0),
     'L1_attn_gn_g': (1.0, 0.6),
     'L1_attn_gn_b': (0.0, 2.0),
     'L1_attn_mn_g': (1.0, 0.6),
     'L1_attn_mn_b': (0.0, 2.0)}
    factors = {'L0_attn_Wk': 8.0,
     'L0_attn_Wv': 8.0,
     'L1_attn_Wq': 46.191,
     'L1_attn_Wk': 60.487,
     'L1_attn_Wv': 200.0,
     'L1_attn_Wo': 40.995,
     'L1_attn_conv_w': 64.0,
     'L1_attn_ig_w': 189.04,
     'L1_attn_og_w': 64.0,
     'L1_attn_gamma_w': 64.0,
     'L1_attn_gamma_b': 64.0}
    for name, (base, spread) in spreads.items():
        noise = np.random.default_rng([zlib.crc32(name.encode()), seed]).standard_normal(out[name].shape)
        drawn = base * np.exp(spread * noise) if base else spread * noise
        out[name] = jnp.asarray(drawn.astype(out[name].dtype))
    for name, factor in factors.items():
        out[name] = (out[name] * factor).astype(out[name].dtype)
    return out
```

```python
from contextlib import ExitStack

import concourse.bass as bass
from concourse import mybir

ALU = mybir.AluOpType
ACT = mybir.ActivationFunctionType
AX_X = mybir.AxisListType.X
F32 = mybir.dt.float32
F32R = mybir.dt.float32r
I32 = mybir.dt.int32
F8 = mybir.dt.float8e4

P = 128
D = 256
KC = D // P
BATCH, SEQ = 8, 256
TOK = BATCH * SEQ
TILES = TOK // P
GROUPS = 4
GT = TOK // GROUPS
TPG = GT // P
BPG = BATCH // GROUPS
EPS = 1e-5

HEADS, QPK, DH = 8, 4, 8
DKV = HEADS * DH
SCALE = float(DH) ** -0.5
UNITS = BPG * HEADS
QKV = D + P + DKV
ROWS = 4 * 3 * DH
C_ID, C_SELQ, C_SELK, C_COL = 0, P, P + 8 * P, P + 16 * P
NCONST = C_COL + 6

START = 1
IN_LOOPS_0 = """k_b_done k_parts_done max_done max_placed max_split max_turned mem_done mem_mm o_normed o_turned
    probs_done proj pv_copied pv_done q_exp_done q_lo_done s_done sel_act sel_dve selected sigma_done
    st_done v_done x_updated xn_hi_done xn_lo_done xn_ready xn_saved xn_turned""".split()
IN_LOOPS_1 = """down_step gate_done gelu_done hid_done hid_hi_done hid_lo_done up_done x_updated y_done y_turned""".split()


def prime(nc, semaphores):
    with nc.Block() as block:
        @block.sync
        def _(sp):
            for s in semaphores:
                sp.sem_inc(s, START)


def layer0_attention(nc, stack, dram, keep):
    X, ident = keep["X"], keep["ident"]
    with ExitStack() as ctx:
        def sb(name, shape, dt=F32):
            return ctx.enter_context(nc.sbuf_tensor(name, shape, dt))

        def sem(name):
            return ctx.enter_context(nc.semaphore(name))

        const = sb("const", [P, NCONST])
        sel_q = sb("sel_q", [P, 8, P], F32R)
        sel_k = sb("sel_k", [P, 8, P], F32R)
        alpha, beta = const[:, C_COL:C_COL + 1], const[:, C_COL + 1:C_COL + 2]
        w_raw = sb("w_raw", [P, KC, QKV])
        w_hi = sb("w_hi", [P, KC, QKV], F32R)
        w_lo = sb("w_lo", [P, KC, QKV], F32R)
        mem2 = sb("mem2", [P, 2, DKV + 1])
        mw = sb("mw", [P, 4])
        stats = sb("stats", [P, TILES, 6])
        mv = sb("mv", [P, TILES, 2])
        rstd = sb("rstd", [P, TILES])
        xn = sb("xn", [P, 2, KC, P])
        xn_hi = sb("xn_hi", [P, KC, GT], F32R)
        xn_lo = sb("xn_lo", [P, KC, GT], F32R)
        q_hi = sb("q_hi", [P, 2, GT], F32R)
        q_lo = sb("q_lo", [P, 2, GT], F32R)
        q_tanh = sb("q_tanh", [P, 2, GT])
        q_rec = sb("q_rec", [P, 2, GT])
        sigma = sb("sigma", [P, 2, GT])
        k_b = sb("k_b", [P, GT], F32R)
        k_parts = sb("k_parts", [P, GT], F32R)
        Q = sb("Q", [P, 2, BPG, QPK, SEQ], F32R)
        K = sb("K", [P, HEADS, GT], F32R)
        V = sb("V", [P, TPG, HEADS, 32])
        neg_max = sb("neg_max", [P, 2, 8])
        max_parts = sb("max_parts", [8, 2, 2, P], F32R)
        probs = sb("probs", [P, 4, 2, 2, 512])
        o_sb = sb("o_sb", [P, 2, 512])
        o_rec = sb("o_rec", [P, 16])
        att = sb("att", [P, TPG, D])
        a_rec = sb("a_rec", [P, 4])
        a_mem = sb("a_mem", [P, D])

        banks = [ctx.enter_context(nc.psum_tensor(f"bank{n}", [P, 512], F32)) for n in range(8)]

        names = """loaded xloaded const_ready zeroed sem_w w_hi_done w_ready mv_ready std_ready rstd_ready mw_exp mw_ready
            xn_ready xn_turned xn_hi_done xn_lo_done xn_saved
            proj q_exp_done q_hi_done q_lo_done k_b_done k_parts_done v_done sigma_done
            selected sel_act sel_dve mem_mm mem_done s_done max_done max_turned max_split max_placed
            st_done probs_done pv_done pv_copied o_turned o_normed x_updated""".split()
        S = {n: sem(f"a_{n}") for n in names}
        prime(nc, [S[n] for n in IN_LOOPS_0])
        block = ctx.enter_context(nc.Block())

        T4, NS = TPG, 4 * UNITS
        PAIRS = UNITS // 2

        @block.sync
        def _(sp):
            sp.dma_start(X[:], dram["x"].rearrange("(n p) d -> p n d", p=P)).then_inc(S["xloaded"], 16)
            sp.dma_start(const[:], dram["const"]).then_inc(S["loaded"], 16)
            sp.dma_start(w_raw[:], dram["wqkv"]).then_inc(S["loaded"], 16)
            sp.wait_ge(S["zeroed"], 1)
            for j in range(2):
                sp.dma_start(mem2[64 * j:64 * j + 64, j, 0:DKV], dram["memory"]).then_inc(S["loaded"], 16)
                sp.dma_start(mem2[64 * j:64 * j + 64, j, DKV:DKV + 1], dram["memory_norm"]).then_inc(S["loaded"], 16)
            sp.dma_start(mw[:, 0:1], dram["memory_weight"].rearrange("(a b) -> a b", a=1).partition_broadcast(P)).then_inc(S["loaded"], 16)

            with sp.Fori(0, GROUPS) as i:
                at = sp.snap(i * GT)
                sp.wait_ge(S["xn_lo_done"], START + i * T4 + T4)
                sp.dma_start(keep["xall_hi"][:, :, bass.ds(at, GT)].bitcast(F32), xn_hi[:].bitcast(F32)).then_inc(S["xn_saved"], 16)
                sp.dma_start(keep["xall_lo"][:, :, bass.ds(at, GT)].bitcast(F32), xn_lo[:].bitcast(F32)).then_inc(S["xn_saved"], 16)
                for u in range(UNITS):
                    h, b = divmod(u, BPG)
                    row = ROWS + 2 * (h % 4)
                    sp.wait_ge(S["max_split"], START + i * UNITS + u + 1)
                    for part in range(2):
                        sp.dma_start(
                            Q[row + part:row + part + 1, h // 4, b, :, :].rearrange("a q (s n) -> a (q s) n", n=P).bitcast(F32),
                            max_parts[:, u % 2, part, :].bitcast(F32),
                        ).then_inc(S["max_placed"], 16)
            sp.wait_ge(S["xn_saved"], START + 32 * GROUPS)

        @block.gpsimd
        def _(pool):
            pool.memset(mem2[:], 0.0).then_inc(S["zeroed"], 1)
            pool.memset(V[:], 0.0).then_inc(S["zeroed"], 1)
            pool.wait_ge(S["zeroed"], 2)
            pool.memset(V[:, :, :, DH:DH + 1], 1.0).then_inc(S["zeroed"], 1)

        @block.scalar
        def _(act):
            act.wait_ge(S["loaded"], 16 * 7)
            act.activation(ident[:], const[:, C_ID:C_ID + P], ACT.Copy).then_inc(S["const_ready"], 1)
            act.activation(sel_q[:].rearrange("p a b -> p (a b)"), const[:, C_SELQ:C_SELQ + 8 * P], ACT.Copy).then_inc(S["const_ready"], 1)
            act.activation(sel_k[:].rearrange("p a b -> p (a b)"), const[:, C_SELK:C_SELK + 8 * P], ACT.Copy).then_inc(S["const_ready"], 1)
            act.activation(w_hi[:], w_raw[:], ACT.Copy).then_inc(S["w_hi_done"], 1)
            act.wait_ge(S["mv_ready"], 1)
            act.activation(rstd[:], mv[:, :, 1], ACT.Sqrt, bias=keep["eps"][:]).then_inc(S["std_ready"], 1)
            act.activation(mw[:, 1:2], mw[:, 0:1], ACT.Exp, scale=-1.0).then_inc(S["mw_exp"], 1)

            with act.Fori(0, GROUPS) as i:
                for t in range(T4):
                    act.wait_ge(S["xn_turned"], START + i * T4 + t + 1)
                    if t == 0:
                        act.wait_ge(S["proj"], START + i * 7)
                        act.wait_ge(S["xn_saved"], START + i * 32)
                    act.activation(xn_hi[:, :, P * t:P * t + P], banks[t % 2][:, 0:D].rearrange("p (k n) -> p k n", k=KC),
                                   ACT.Copy).then_inc(S["xn_hi_done"], 1)
                for c in range(2):
                    act.wait_ge(S["proj"], START + i * 7 + c + 1)
                    act.activation(q_hi[:, c, :], banks[2 + c][:], ACT.Copy).then_inc(S["q_hi_done"], 1)
                    act.activation(q_tanh[:, c, :], banks[2 + c][:], ACT.Tanh, scale=0.5).then_inc(S["q_exp_done"], 1)
                act.wait_ge(S["proj"], START + i * 7 + 3)
                act.activation(k_b[:], banks[4][:], ACT.Identity, scale=beta).then_inc(S["k_b_done"], 1)
                act.wait_ge(S["proj"], START + i * 7 + 7)
                for t in range(TPG):
                    act.activation(V[:, t, :, 0:DH], banks[5][:, DKV * t:DKV * t + DKV].rearrange("p (h d) -> p h d", h=HEADS),
                                   ACT.Copy).then_inc(S["v_done"], 1)
                for n in range(16):
                    if n % 2 == 0:
                        act.wait_ge(S["selected"], START + i * 16 + n + 1)
                        h = n // 2
                        act.activation(K[:, h, :], banks[n % 4][:], ACT.Identity,
                                       bias=const[:, C_COL + 2 + h % 4:C_COL + 3 + h % 4]).then_inc(S["sel_act"], 1)
                for slot in range(UNITS + 3):
                    if slot < UNITS:
                        u = slot
                        for j in range(4):
                            act.wait_ge(S["st_done"], START + i * NS + 4 * u + j + 1)
                            if j == 0 and u >= 4:
                                act.wait_ge(S["pv_done"], START + i * PAIRS + (u - 4) // 2 + 1)
                            act.activation(probs[:, u % 4, j // 2, j % 2, :], banks[2 + j % 2][:], ACT.Exp,
                                           scale=SCALE).then_inc(S["probs_done"], 1)
                    if slot >= 2 and slot % 2 == 0 and slot <= UNITS:
                        pr = slot // 2 - 1
                        act.wait_ge(S["pv_done"], START + i * PAIRS + pr + 1)
                        if pr >= 2:
                            act.wait_ge(S["o_turned"], START + i * PAIRS + pr - 1)
                        act.activation(o_sb[:, pr % 2, :], banks[4 + pr % 2][:], ACT.Copy).then_inc(S["pv_copied"], 1)

        @block.vector
        def _(dve):
            dve.wait_ge(S["xloaded"], 16)
            for t in range(TILES):
                dve.bn_stats(stats[:, t, :], X[:, t, :]).then_inc(S["sem_w"], 1)
            for t in range(TILES):
                dve.wait_ge(S["sem_w"], t + 1)
                last = dve.bn_aggr(mv[:, t, :], stats[:, t, :])
            last.then_inc(S["mv_ready"], 1)
            dve.wait_ge(S["w_hi_done"], 1)
            dve.tensor_tensor(w_lo[:], w_raw[:], w_hi[:].bitcast(F32), ALU.subtract).then_inc(S["w_ready"], 1)
            dve.wait_ge(S["std_ready"], 1)
            dve.reciprocal(rstd[:], rstd[:]).then_inc(S["rstd_ready"], 1)
            dve.wait_ge(S["mw_exp"], 1)
            dve.tensor_scalar(mw[:, 2:3], mw[:, 1:2], 1.0, None, ALU.add).then_inc(S["mw_ready"], 1)
            dve.wait_ge(S["mw_ready"], 1)
            dve.reciprocal(mw[:, 2:3], mw[:, 2:3]).then_inc(S["mw_ready"], 1)
            dve.wait_ge(S["mw_ready"], 2)
            dve.tensor_scalar(mw[:, 3:4], mw[:, 2:3], -1.0, 1.0, ALU.mult, ALU.add).then_inc(S["mw_ready"], 1)
            dve.wait_ge(S["mw_ready"], 3)
            dve.wait_ge(S["rstd_ready"], 1)
            dve.wait_ge(S["const_ready"], 3)

            with dve.Fori(0, GROUPS) as i:
                def normalise(t):
                    if t >= 2:
                        dve.wait_ge(S["xn_turned"], START + i * T4 + t - 1)
                    else:
                        dve.wait_ge(S["xn_turned"], START + i * T4)
                    mean = mv[:, bass.ds(i * TPG + t, 1), 0]
                    dve.tensor_scalar(xn[:, t % 2, :, :], X[:, bass.ds(i * TPG + t, 1), :].rearrange("p a (j k) -> p (a k) j", k=KC),
                                      mean, rstd[:, bass.ds(i * TPG + t, 1)], ALU.subtract, ALU.mult).then_inc(S["xn_ready"], 1)

                normalise(0)
                for t in range(T4):
                    if t + 1 < T4:
                        normalise(t + 1)
                    dve.wait_ge(S["xn_hi_done"], START + i * T4 + t + 1)
                    dve.tensor_tensor(xn_lo[:, :, P * t:P * t + P], banks[t % 2][:, 0:D].rearrange("p (k n) -> p k n", k=KC),
                                      xn_hi[:, :, P * t:P * t + P].bitcast(F32), ALU.subtract).then_inc(S["xn_lo_done"], 1)
                for c in range(2):
                    dve.wait_ge(S["q_exp_done"], START + i * 2 + c + 1)
                    dve.tensor_tensor(q_lo[:, c, :], banks[2 + c][:], q_hi[:, c, :].bitcast(F32), ALU.subtract).then_inc(S["q_lo_done"], 1)
                    dve.tensor_scalar(q_tanh[:, c, :], q_tanh[:, c, :], 0.0, -1.0, ALU.min, ALU.mult).then_inc(S["sigma_done"], 1)
                dve.wait_ge(S["k_b_done"], START + i + 1)
                dve.scalar_tensor_tensor(out=k_parts[:], in0=banks[4][:], scalar=alpha, in1=k_b[:].bitcast(F32),
                                         op0=ALU.mult, op1=ALU.add).then_inc(S["k_parts_done"], 1)
                dve.wait_ge(S["sigma_done"], START + i * 8 + 2)
                dve.tensor_scalar(q_rec[:], q_tanh[:], 1.0, None, ALU.add).then_inc(S["sigma_done"], 1)
                dve.wait_ge(S["sigma_done"], START + i * 8 + 3)
                dve.reciprocal(q_rec[:], q_rec[:]).then_inc(S["sigma_done"], 1)
                dve.wait_ge(S["sigma_done"], START + i * 8 + 4)
                for c in range(2):
                    dve.scalar_tensor_tensor(out=q_tanh[:, c, :], in0=q_tanh[:, c, :], scalar=-2.0, in1=q_rec[:, c, :],
                                             op0=ALU.mult, op1=ALU.mult).then_inc(S["sigma_done"], 1)
                dve.wait_ge(S["sigma_done"], START + i * 8 + 6)
                for c in range(2):
                    dve.scalar_tensor_tensor(out=sigma[:, c, :], in0=banks[2 + c][:], scalar=0.0, in1=q_tanh[:, c, :],
                                             op0=ALU.max, op1=ALU.add).then_inc(S["sigma_done"], 1)
                for n in range(16):
                    if n % 2 == 1:
                        dve.wait_ge(S["selected"], START + i * 16 + n + 1)
                        m = n // 2
                        dve.tensor_copy(Q[:, m // QPK, :, m % QPK, :], banks[n % 4][:].rearrange("p (b s) -> p b s", b=BPG)).then_inc(S["sel_dve"], 1)
                for t in range(TPG):
                    am = banks[6 + t % 2][:, 0:2 * 2 * (DKV + 1)].rearrange("p (q n) -> p q n", n=DKV + 1)
                    dve.wait_ge(S["mem_mm"], START + i * TPG + t + 1)
                    if t == 0:
                        dve.wait_ge(S["mem_done"], START + i * 3 * TPG)
                    else:
                        dve.wait_ge(S["mem_done"], START + i * 3 * TPG + 3 * t)
                    dve.reciprocal(a_rec[:], am[:, :, DKV]).then_inc(S["mem_done"], 1)
                    dve.wait_ge(S["mem_done"], START + i * 3 * TPG + 3 * t + 1)
                    dve.tensor_tensor(a_mem[:].rearrange("p (q n) -> p q n", n=DKV), am[:, :, 0:DKV],
                                      a_rec[:].rearrange("p (q n) -> p q n", n=1).to_broadcast([P, 4, DKV]),
                                      ALU.mult).then_inc(S["mem_done"], 1)
                    dve.wait_ge(S["mem_done"], START + i * 3 * TPG + 3 * t + 2)
                    xt = X[:, bass.ds(i * TPG + t, 1), :].rearrange("p a d -> p (a d)")
                    dve.scalar_tensor_tensor(out=xt, in0=a_mem[:], scalar=mw[:, 2:3], in1=xt,
                                             op0=ALU.mult, op1=ALU.add).then_inc(S["mem_done"], 1)

                def turned_max(u):
                    dve.wait_ge(S["max_turned"], START + i * UNITS + u + 1)
                    if u >= 2:
                        dve.wait_ge(S["max_placed"], START + i * 32 * UNITS + 32 * (u - 1))
                    else:
                        dve.wait_ge(S["max_placed"], START + i * 32 * UNITS)
                    if u >= 2:
                        dve.wait_ge(S["st_done"], START + i * NS + 4 * (u - 1))
                    dve.tensor_copy(max_parts[:, u % 2, 0, :], banks[6][0:8, 0:P]).then_inc(S["sem_w"], 1)
                    dve.wait_ge(S["sem_w"], TILES + i * UNITS + u + 1)
                    dve.tensor_tensor(max_parts[:, u % 2, 1, :], banks[6][0:8, 0:P], max_parts[:, u % 2, 0, :].bitcast(F32),
                                      ALU.subtract).then_inc(S["max_split"], 1)

                for slot in range(-2, UNITS + 2):
                    u = slot + 2
                    if u < UNITS:
                        for j in range(4):
                            dve.wait_ge(S["s_done"], START + i * NS + 4 * u + j + 1)
                            if j == 0 and u >= 2:
                                dve.wait_ge(S["max_turned"], START + i * UNITS + u - 1)
                            dve.tensor_reduce(neg_max[:, u % 2, 2 * j:2 * j + 2], banks[j % 2][:].rearrange("p (s n) -> p s n", s=2),
                                              AX_X, ALU.max, negate=True).then_inc(S["max_done"], 1)
                            if j == 1 and u >= 1:
                                turned_max(u - 1)
                    elif u == UNITS:
                        turned_max(UNITS - 1)
                    if slot >= 3 and slot % 2 == 1:
                        pr = (slot - 3) // 2
                        ot = banks[7][:].rearrange("p (l s g c) -> p l s g c", l=2, s=2, g=4)
                        dve.wait_ge(S["o_turned"], START + i * PAIRS + pr + 1)
                        dve.wait_ge(S["o_normed"], START + i * 5 * PAIRS + 5 * pr)
                        dve.reciprocal(o_rec[:], banks[7][:].rearrange("p (g c) -> p g c", c=32)[:, :, DH]).then_inc(S["o_normed"], 1)
                        dve.wait_ge(S["o_normed"], START + i * 5 * PAIRS + 5 * pr + 1)
                        rec = o_rec[:].rearrange("p (l s g a) -> p l s g a", l=2, s=2, a=1)
                        for s in range(2):
                            for v in range(2):
                                h, b = divmod(2 * pr + v, BPG)
                                out = att[:, 2 * b + s, :].rearrange("p (g l h d) -> p l g h d", g=2, l=2, h=HEADS)[:, :, :, h, :]
                                dve.tensor_tensor(out, ot[:, :, s, 2 * v:2 * v + 2, 0:DH],
                                                  rec[:, :, s, 2 * v:2 * v + 2, :].to_broadcast([P, 2, 2, DH]),
                                                  ALU.mult).then_inc(S["o_normed"], 1)
                dve.wait_ge(S["o_normed"], START + i * 5 * PAIRS + 5 * PAIRS)
                xg = X[:, bass.ds(i * TPG, TPG), :]
                dve.scalar_tensor_tensor(out=xg, in0=att[:], scalar=mw[:, 3:4], in1=xg, op0=ALU.mult, op1=ALU.add).then_inc(S["x_updated"], 1)
                dve.wait_ge(S["x_updated"], START + i + 1)

        @block.tensor
        def _(pe):
            pe.wait_ge(S["const_ready"], 3)
            pe.wait_ge(S["w_ready"], 1)
            pe.wait_ge(S["zeroed"], 3)
            pe.wait_ge(S["loaded"], 16 * 7)

            with pe.Fori(0, GROUPS) as i:
                for t in range(T4):
                    pe.wait_ge(S["xn_ready"], START + i * T4 + t + 1)
                    if t >= 2:
                        pe.wait_ge(S["xn_lo_done"], START + i * T4 + t - 1)
                    elif t == 0:
                        pe.wait_ge(S["max_done"], START + i * NS)
                    for k in range(KC):
                        mm = pe.transpose(banks[t % 2][:, P * k:P * k + P], xn[:, t % 2, k, :], ident[:])
                    mm.then_inc(S["xn_turned"], 1)
                pe.wait_ge(S["xn_lo_done"], START + i * T4 + T4)

                def product(out, cols, moving):
                    n = 0
                    for w, x in ((w_hi, xn_hi), (w_lo, xn_hi), (w_hi, xn_lo)):
                        for k in range(KC):
                            wk, xk = w[:, k, cols], x[:, k, moving]
                            lhs, rhs = (wk, xk) if moving == slice(0, GT) else (xk, wk)
                            mm = pe.matmul(out, lhs, rhs, start=(n == 0), stop=(n == 3 * KC - 1))
                            n += 1
                    mm.then_inc(S["proj"], 1)

                pe.wait_ge(S["probs_done"], START + i * NS)
                pe.wait_ge(S["pv_copied"], START + i * PAIRS)
                for c in range(2):
                    product(banks[2 + c][:], slice(P * c, P * c + P), slice(0, GT))
                product(banks[4][:], slice(D, D + P), slice(0, GT))
                for t in range(TPG):
                    product(banks[5][:, DKV * t:DKV * t + DKV], slice(D + P, QKV), slice(P * t, P * t + P))
                pe.wait_ge(S["q_lo_done"], START + i * 2 + 2)
                pe.wait_ge(S["k_parts_done"], START + i + 1)
                pe.wait_ge(S["sigma_done"], START + i * 8 + 8)
                for n in range(16):
                    if n >= 4:
                        if n % 2 == 0:
                            pe.wait_ge(S["sel_act"], START + i * 8 + n // 2 - 1)
                        else:
                            pe.wait_ge(S["sel_dve"], START + i * 8 + n // 2 - 1)
                    m = n // 2
                    if n % 2 == 0:
                        pe.matmul(banks[n % 4][:], sel_k[:, m, :], k_parts[:], start=True, stop=True).then_inc(S["selected"], 1)
                    else:
                        quad, q = divmod(m, QPK)
                        v = 2 * (2 * quad + q % 2)
                        pe.matmul(banks[n % 4][:], sel_q[:, v, :], q_hi[:, q // 2, :], start=True, stop=False)
                        pe.matmul(banks[n % 4][:], sel_q[:, v + 1, :], q_lo[:, q // 2, :], start=False, stop=True).then_inc(S["selected"], 1)
                for t in range(TPG):
                    if t == 0:
                        pe.wait_ge(S["o_normed"], START + i * 5 * PAIRS)
                        pe.wait_ge(S["max_split"], START + i * UNITS)
                    if t >= 2:
                        pe.wait_ge(S["mem_done"], START + i * 3 * TPG + 3 * (t - 1))
                    for c in range(2):
                        mm = pe.matmul(banks[6 + t % 2][:, 2 * (DKV + 1) * c:2 * (DKV + 1) * (c + 1)],
                                       sigma[:, c, P * t:P * t + P], mem2[:].rearrange("p a b -> p (a b)"), start=True, stop=True)
                    mm.then_inc(S["mem_mm"], 1)
                pe.wait_ge(S["sel_act"], START + i * 8 + 8)
                pe.wait_ge(S["sel_dve"], START + i * 8 + 8)
                pe.wait_ge(S["v_done"], START + i * TPG + TPG)
                pe.wait_ge(S["mem_done"], START + i * 3 * TPG + 3 * TPG)

                def scores(u, j):
                    h, b = divmod(u, BPG)
                    n = 4 * u + j
                    if n >= 2:
                        pe.wait_ge(S["max_done"], START + i * NS + n - 1)
                    for s in range(2):
                        mm = pe.matmul(banks[j % 2][:, SEQ * s:SEQ * s + SEQ], Q[0:ROWS, h // 4, b, j, P * s:P * s + P],
                                       K[0:ROWS, h, SEQ * b:SEQ * b + SEQ], start=True, stop=True)
                    mm.then_inc(S["s_done"], 1)

                def turn_max(u):
                    pe.wait_ge(S["max_done"], START + i * NS + 4 * u + 4)
                    if u >= 1:
                        pe.wait_ge(S["max_split"], START + i * UNITS + u)
                    pe.transpose(banks[6][0:8, 0:P], neg_max[:, u % 2, :], ident[:]).then_inc(S["max_turned"], 1)

                def scores_turned(u, j):
                    h, b = divmod(u, BPG)
                    n = 4 * u + j
                    if j == 0:
                        pe.wait_ge(S["max_placed"], START + i * 32 * UNITS + 32 * (u + 1))
                    if n >= 2:
                        pe.wait_ge(S["probs_done"], START + i * NS + n - 1)
                    th, qp = divmod(j, 2)
                    pe.matmul(banks[2 + j % 2][:].rearrange("p (q n) -> p q n", q=2), K[0:ROWS + 8, h, SEQ * b + P * th:SEQ * b + P * th + P],
                              Q[0:ROWS + 8, h // 4, b, 2 * qp:2 * qp + 2, :], start=True, stop=True).then_inc(S["st_done"], 1)

                def weighted(pr):
                    pe.wait_ge(S["probs_done"], START + i * NS + 8 * pr + 8)
                    if pr >= 2:
                        pe.wait_ge(S["pv_copied"], START + i * PAIRS + pr - 1)
                    for th in range(2):
                        for g in range(4):
                            u = 2 * pr + g // 2
                            h, b = divmod(u, BPG)
                            mm = pe.matmul(banks[4 + pr % 2][32 * g:32 * g + 32, :], V[:, 2 * b + th, h, :],
                                           probs[:, u % 4, th, g % 2, :], start=(th == 0), stop=(th == 1),
                                           skip_group_check=True)
                    mm.then_inc(S["pv_done"], 1)

                def turn_out(pr):
                    pe.wait_ge(S["pv_copied"], START + i * PAIRS + pr + 1)
                    pe.wait_ge(S["o_normed"], START + i * 5 * PAIRS + 5 * pr)
                    for c in range(4):
                        mm = pe.transpose(banks[7][:, P * c:P * c + P], o_sb[:, pr % 2, P * c:P * c + P], ident[:])
                    mm.then_inc(S["o_turned"], 1)

                for slot in range(-2, UNITS + 2):
                    for j in range(4):
                        if slot + 2 < UNITS:
                            scores(slot + 2, j)
                        if j == 1 and 0 <= slot + 1 < UNITS:
                            turn_max(slot + 1)
                        if 0 <= slot < UNITS:
                            scores_turned(slot, j)
                    if slot >= 2 and slot % 2 == 0 and slot <= UNITS:
                        weighted(slot // 2 - 1)
                    if slot >= 3 and slot % 2 == 1:
                        turn_out((slot - 3) // 2)


NVFP_BLOCK = 32
MLP = 2048
PAIRS_N = MLP // (2 * P)
WORDS = 3 * D
CHUNKS = MLP // P


def layer0_mlp(nc, dram, keep):
    X, ident, x_hi, x_lo = keep["X"], keep["ident"], keep["xall_hi"], keep["xall_lo"]
    with ExitStack() as ctx:
        def sb(name, shape, dt=F32):
            return ctx.enter_context(nc.sbuf_tensor(name, shape, dt))

        codes = sb("codes", [P, 2, WORDS], I32)
        scales = sb("scales", [P, 2, WORDS])
        bits_a = sb("bits_a", [P, WORDS], I32)
        bits_b = sb("bits_b", [P, WORDS], I32)
        w = sb("w", [P, 2, 2, WORDS])
        w_hi = sb("w2_hi", [P, PAIRS_N, 2, WORDS], F32R)
        w_lo = sb("w2_lo", [P, PAIRS_N, 2, WORDS], F32R)
        gelu = sb("gelu", [P, 2, GT])
        hid = sb("hid", [P, 2, GT])
        hid_hi = sb("hid_hi", [P, 2, GT], F32R)
        hid_lo = sb("hid_lo", [P, 2, GT], F32R)
        y = sb("y", [P, KC, GT])

        banks = [ctx.enter_context(nc.psum_tensor(f"mbank{n}", [P, 512], F32)) for n in range(8)]
        gate_b, up_b, down_b, turn_b = banks[0:2], banks[2:4], banks[4:6], banks[6:8]
        names = """code_even code_odd decoded w_done w_hi_done w_lo_done gate_done up_done gelu_done hid_done
            hid_hi_done hid_lo_done down_step y_done y_turned x_updated""".split()
        S = {n: ctx.enter_context(nc.semaphore(f"m_{n}")) for n in names}
        prime(nc, [S[n] for n in IN_LOOPS_1])
        code_sem = [S["code_even"], S["code_odd"]]
        block = ctx.enter_context(nc.Block())
        C = CHUNKS

        @block.sync
        def _(sp):
            for a in range(PAIRS_N):
                if a >= 2:
                    sp.wait_ge(S["w_done"], a - 1)
                sp.dma_start(codes[:, a % 2, :], dram["codes"][:, a, :]).then_inc(code_sem[a % 2], 16)
                sp.dma_start(scales[:, a % 2, :], dram["scales"][:, a, :]).then_inc(code_sem[a % 2], 16)

        def decode(dve, a):
            c, s = codes[:, a % 2, :], scales[:, a % 2, :]
            n = 5 * a
            dve.wait_ge(code_sem[a % 2], 32 * (a // 2 + 1))
            dve.tensor_scalar(bits_a[:], c, 4, 0xF00, ALU.logical_shift_left, ALU.bitwise_and).then_inc(S["decoded"], 1)
            dve.wait_ge(S["decoded"], n + 1)
            dve.scalar_tensor_tensor(out=bits_b[:], in0=c, scalar=0xF, in1=bits_a[:],
                                     op0=ALU.bitwise_and, op1=ALU.bitwise_or).then_inc(S["decoded"], 1)
            dve.wait_ge(S["decoded"], n + 2)
            dve.tensor_scalar(bits_a[:], bits_b[:], 0x808, 4, ALU.bitwise_and, ALU.logical_shift_left).then_inc(S["decoded"], 1)
            dve.tensor_scalar(bits_b[:], bits_b[:], 0x707, 2, ALU.bitwise_and, ALU.logical_shift_left).then_inc(S["decoded"], 1)
            dve.wait_ge(S["decoded"], n + 4)
            dve.tensor_tensor(bits_b[:], bits_b[:], bits_a[:], ALU.bitwise_or).then_inc(S["decoded"], 1)
            dve.wait_ge(S["decoded"], n + 5)
            if a >= 2:
                dve.wait_ge(S["w_lo_done"], a - 1)
            values = bits_b[:].bitcast(F8).rearrange("p (n b) -> p b n", b=4)
            dve.scalar_tensor_tensor(out=w[:, a % 2, 0, :], in0=values[:, 0, :], scalar=64.0, in1=s, op0=ALU.mult, op1=ALU.mult)
            dve.scalar_tensor_tensor(out=w[:, a % 2, 1, :], in0=values[:, 1, :], scalar=64.0, in1=s,
                                     op0=ALU.mult, op1=ALU.mult).then_inc(S["w_done"], 1)

        @block.gpsimd
        def _(pool):
            for a in range(PAIRS_N):
                pool.wait_ge(S["w_hi_done"], a + 1)
                pool.tensor_tensor(w_lo[:, a, :, :], w[:, a % 2, :, :], w_hi[:, a, :, :].bitcast(F32), ALU.subtract).then_inc(S["w_lo_done"], 1)

        @block.vector
        def _(dve):
            def turn(i, first):
                def hidden(c):
                    dve.wait_ge(S["gelu_done"], START + i * C + c + 1)
                    dve.wait_ge(S["up_done"], START + i * C + c + 1)
                    if c >= 2:
                        dve.wait_ge(S["hid_lo_done"], START + i * C + c - 1)
                    dve.tensor_tensor(hid[:, c % 2, :], gelu[:, c % 2, :], up_b[c % 2][:], ALU.mult).then_inc(S["hid_done"], 1)

                def hidden_lo(c):
                    dve.wait_ge(S["hid_hi_done"], START + i * C + c + 1)
                    dve.tensor_tensor(hid_lo[:, c % 2, :], hid[:, c % 2, :], hid_hi[:, c % 2, :].bitcast(F32),
                                      ALU.subtract).then_inc(S["hid_lo_done"], 1)

                for c in range(C):
                    if c >= 1:
                        hidden_lo(c - 1)
                    hidden(c)
                    if first and c % 2 == 0 and c // 2 + 2 < PAIRS_N:
                        decode(dve, c // 2 + 2)
                hidden_lo(C - 1)
                for t in range(TPG):
                    dve.wait_ge(S["y_turned"], START + i * TPG + t + 1)
                    xt = X[:, bass.ds(i * TPG + t, 1), :].rearrange("p a d -> p (a d)")
                    dve.tensor_tensor(xt, turn_b[t % 2][:, 0:D], xt, ALU.add).then_inc(S["x_updated"], 1)

            decode(dve, 0)
            decode(dve, 1)
            turn(0, True)
            with dve.Fori(1, GROUPS) as i:
                turn(i, False)

        @block.scalar
        def _(act):
            def turn(i, first):
                def hidden_hi(c):
                    act.wait_ge(S["hid_done"], START + i * C + c + 1)
                    if c >= 2:
                        act.wait_ge(S["down_step"], START + i * C + c - 1)
                    act.activation(hid_hi[:, c % 2, :], hid[:, c % 2, :], ACT.Copy).then_inc(S["hid_hi_done"], 1)

                for c in range(C):
                    if c >= 1:
                        hidden_hi(c - 1)
                    act.wait_ge(S["gate_done"], START + i * C + c + 1)
                    if c >= 2:
                        act.wait_ge(S["hid_done"], START + i * C + c - 1)
                    act.activation(gelu[:, c % 2, :], gate_b[c % 2][:], ACT.Gelu_apprx_tanh).then_inc(S["gelu_done"], 1)
                    if first and c % 2 == 0 and c // 2 + 2 < PAIRS_N:
                        weights_hi(c // 2 + 2)
                hidden_hi(C - 1)
                for k in range(KC):
                    act.wait_ge(S["down_step"], START + i * C + C)
                    act.activation(y[:, k, :], down_b[k][:], ACT.Copy).then_inc(S["y_done"], 1)

            def weights_hi(a):
                act.wait_ge(S["w_done"], a + 1)
                act.activation(w_hi[:, a, :, :], w[:, a % 2, :, :], ACT.Copy).then_inc(S["w_hi_done"], 1)

            weights_hi(0)
            weights_hi(1)
            turn(0, True)
            with act.Fori(1, GROUPS) as i:
                turn(i, False)

        @block.tensor
        def _(pe):
            with pe.Fori(0, GROUPS) as i:
                def up(c, which, bank, done):
                    a, m = divmod(c, 2)
                    cols = slice(D * which + P * m, D * which + P * m + P)
                    n = 0
                    for wt, x in ((w_hi, x_hi), (w_lo, x_hi), (w_hi, x_lo)):
                        for k in range(KC):
                            mm = pe.matmul(bank[:], wt[:, a, k, cols], x[:, k, bass.ds(i * GT, GT)], start=(n == 0), stop=(n == 5))
                            n += 1
                    mm.then_inc(done, 1)

                def down(c):
                    a, m = divmod(c, 2)
                    pe.wait_ge(S["hid_lo_done"], START + i * C + c + 1)
                    if c == 0:
                        pe.wait_ge(S["y_done"], START + i * KC)
                    for k in range(KC):
                        cols = slice(2 * D + P * k, 2 * D + P * k + P)
                        for n, (wt, h) in enumerate(((w_hi, hid_hi), (w_lo, hid_hi), (w_hi, hid_lo))):
                            mm = pe.matmul(down_b[k][:], wt[:, a, m, cols], h[:, c % 2, :],
                                           start=(c == 0 and n == 0), stop=(c == C - 1 and n == 2))
                    mm.then_inc(S["down_step"], 1)

                for c in range(C):
                    pe.wait_ge(S["w_lo_done"], c // 2 + 1)
                    if c >= 2:
                        pe.wait_ge(S["gelu_done"], START + i * C + c - 1)
                    up(c, 0, gate_b[c % 2], S["gate_done"])
                    if c >= 2:
                        pe.wait_ge(S["hid_done"], START + i * C + c - 1)
                    up(c, 1, up_b[c % 2], S["up_done"])
                    if c >= 1:
                        down(c - 1)
                down(C - 1)
                for t in range(TPG):
                    if t == 0:
                        pe.wait_ge(S["y_done"], START + i * KC + KC)
                        pe.wait_ge(S["x_updated"], START + i * TPG)
                    if t >= 2:
                        pe.wait_ge(S["x_updated"], START + i * TPG + t - 1)
                    for k in range(KC):
                        mm = pe.transpose(turn_b[t % 2][:, P * k:P * k + P], y[:, k, P * t:P * t + P], ident[:])
                    mm.then_inc(S["y_turned"], 1)


L1_HEADS, L1_DH, TAPS = 16, 16, 4
PAD = TAPS - 1
FFN, FFN_CHUNKS = 704, 6
C2_E, C2_CENTER, C2_COL = 0, P, 2 * P
N_CONST2 = 2 * P + 2
W_QK, W_V, W_IO, W_G, W_COLS = 0, 2 * D, 3 * D, 5 * D, 6 * D
G16, G256 = 4 * L1_DH, 2 * D


def layer1(nc, dram, keep, out):
    X, ident = keep["X"], keep["ident"]
    with ExitStack() as ctx:
        def sb(name, shape, dt=F32):
            return ctx.enter_context(nc.sbuf_tensor(name, shape, dt))

        const2 = sb("const2", [P, N_CONST2])
        ones_rows = sb("ones_rows", [P, P], F32R)
        all_ones = sb("all_ones", [P, P])
        center = const2[:, C2_CENTER:C2_CENTER + P]
        w_hi = sb("l1_hi", [P, KC, W_COLS], F32R)
        w_lo = sb("l1_lo", [P, KC, W_COLS], F32R)
        wo_hi = sb("wo_hi", [P, KC, D], F32R)
        wo_lo = sb("wo_lo", [P, KC, D], F32R)
        bias = sb("bias", [P, 2 * D], F32R)
        conv = sb("conv", [P, KC, TAPS + 1])
        gamma_b = sb("gamma_b", [P, KC])
        par = sb("par", [P, G16 + G256])
        vn_g, vn_b, mn_g, mn_b = (par[:, L1_DH * n:L1_DH * n + L1_DH].rearrange("p (a d) -> p a d", a=1)
                                  .to_broadcast([P, L1_HEADS, L1_DH]) for n in range(4))
        gn_g, gn_b = par[:, G16:G16 + D], par[:, G16 + D:G16 + 2 * D]
        UPC = KC * FFN_CHUNKS * P
        tern = sb("tern", [P, 2 * UPC + FFN_CHUNKS * D], F32R)
        parts = [slice(0, UPC), slice(UPC, 2 * UPC), slice(2 * UPC, 2 * UPC + FFN_CHUNKS * D)]
        w1 = tern[:, parts[0]].rearrange("p (k n) -> p k n", k=KC)
        w2 = tern[:, parts[1]].rearrange("p (k n) -> p k n", k=KC)
        w3 = tern[:, parts[2]].rearrange("p (c n) -> p c n", n=D)
        half = sb("half", [P, 48])
        eps16 = sb("eps16", [P, 48])
        stats = sb("l1_stats", [P, TILES, 6])
        mv = sb("l1_mv", [P, TILES, 2])
        rstd = sb("l1_rstd", [P, TILES])
        with ExitStack() as prep:
            def tmp(name, shape, dt=F32):
                return prep.enter_context(nc.sbuf_tensor(name, shape, dt))

            w_raw = tmp("l1_raw", [P, KC, W_COLS])
            v_sum = tmp("v_sum", [P, KC, L1_HEADS])
            wo_raw = tmp("wo_raw", [P, KC, D])
            bias_raw = tmp("bias_raw", [P, 2 * D])
            bias_b = tmp("bias_b", [P, 2 * D], F32R)
            t_raw = tmp("t_raw", [P, 2 * UPC + FFN_CHUNKS * D])
            below_r = tmp("below_r", [P, UPC])
            t_sum = tmp("t_sum", [P, 3])
            t_thr = tmp("t_thr", [P, 6])
            sums = prep.enter_context(nc.psum_tensor("sums", [P, 512], F32))
            once = {n: prep.enter_context(nc.semaphore(f"l1_{n}")) for n in
                    "loaded zeroed v_centered w_hi_done w_lo_done bias_b_done bias_done t_summed t_spread thr ternary_step ternary stats_done mv_done var_done rstd_done scaled".split()}
            block = prep.enter_context(nc.Block())

            def each(ap, n=L1_HEADS):
                return ap.rearrange("p (h a) -> p h a", a=1).to_broadcast([P, n, L1_DH])

            @block.sync
            def _(sp):
                sp.wait_ge(once["zeroed"], 1)
                loads = [(const2[:], dram["const2"]), (w_raw[:], dram["l1w"]), (wo_raw[:], dram["wo"]), (t_raw[:], dram["ternary"]),
                         (conv[:], dram["conv"]), (gamma_b[:], dram["gamma_b"])]
                for n, name in enumerate(("vn_g", "vn_b", "mn_g", "mn_b")):
                    loads.append((par[:, L1_DH * n:L1_DH * n + L1_DH], dram[name].rearrange("(a d) -> a d", a=1).partition_broadcast(P)))
                for n, name in enumerate(("gn_g", "gn_b")):
                    loads.append((par[:, G16 + D * n:G16 + D * n + D], dram[name].rearrange("(a d) -> a d", a=1).partition_broadcast(P)))
                for row in range(2):
                    for n, name in enumerate(("ig_b", "og_b")):
                        loads.append((bias_raw[row:row + 1, D * n:D * n + D], dram[name].rearrange("(a d) -> a d", a=1)))
                assert len(loads) == N_LOADS
                for dst, src in loads:
                    sp.dma_start(dst, src).then_inc(once["loaded"], 16)

            @block.gpsimd
            def _(pool):
                pool.memset(bias_raw[:], 0.0).then_inc(once["zeroed"], 1)
                pool.memset(half[:], -0.5).then_inc(once["zeroed"], 1)
                pool.memset(eps16[:, 0:32], 0.0).then_inc(once["zeroed"], 1)
                pool.memset(eps16[:, 32:48], L1_DH * EPS).then_inc(once["zeroed"], 1)
                pool.memset(all_ones[:], 1.0).then_inc(once["zeroed"], 1)
                pool.wait_ge(once["zeroed"], 5)
                pool.wait_ge(once["mv_done"], 1)
                pool.tensor_scalar(rstd[:], mv[:, :, 1], 1.0, EPS, ALU.mult, ALU.add).then_inc(once["var_done"], 1)
                pool.wait_ge(once["var_done"], 1)
                pool.tensor_tensor(rstd[:], rstd[:], half[:, 0:TILES], ALU.pow).then_inc(once["rstd_done"], 1)
                pool.wait_ge(once["loaded"], 16 * N_LOADS)
                for n in (0, 2):
                    scale = par[:, L1_DH * n:L1_DH * n + L1_DH]
                    pool.tensor_scalar(scale, scale, 4.0, None, ALU.mult).then_inc(once["scaled"], 1)
                pool.tensor_scalar(gn_g, gn_g, 4.0, None, ALU.mult).then_inc(once["scaled"], 1)
                pool.wait_ge(once["w_hi_done"], 2)
                pool.tensor_tensor(w_lo[:], w_raw[:], w_hi[:].bitcast(F32), ALU.subtract).then_inc(once["w_lo_done"], 1)
                pool.tensor_tensor(wo_lo[:], wo_raw[:], wo_hi[:].bitcast(F32), ALU.subtract).then_inc(once["w_lo_done"], 1)


            @block.scalar
            def _(act):
                act.wait_ge(once["loaded"], 16 * N_LOADS)
                act.activation(ones_rows[:], const2[:, C2_E:C2_E + P], ACT.Copy).then_inc(once["bias_b_done"], 1)
                act.activation(bias_b[:], bias_raw[:], ACT.Identity, scale=const2[:, C2_COL + 1:C2_COL + 2]).then_inc(once["bias_b_done"], 1)
                act.wait_ge(once["v_centered"], 3)
                act.activation(w_hi[:], w_raw[:], ACT.Copy).then_inc(once["w_hi_done"], 1)
                act.activation(wo_hi[:], wo_raw[:], ACT.Copy).then_inc(once["w_hi_done"], 1)


            @block.vector
            def _(dve):
                for t in range(TILES):
                    dve.bn_stats(stats[:, t, :], X[:, t, :]).then_inc(once["stats_done"], 1)
                for t in range(TILES):
                    dve.wait_ge(once["stats_done"], t + 1)
                    ins = dve.bn_aggr(mv[:, t, :], stats[:, t, :])
                ins.then_inc(once["mv_done"], 1)
                dve.wait_ge(once["loaded"], 16 * N_LOADS)
                wv = w_raw[:, :, W_V:W_V + D].rearrange("p k (h d) -> p k h d", d=L1_DH)
                dve.tensor_reduce(v_sum[:], wv, AX_X, ALU.add).then_inc(once["v_centered"], 1)
                dve.wait_ge(once["v_centered"], 1)
                for k in range(KC):
                    dve.scalar_tensor_tensor(out=wv[:, k], in0=each(v_sum[:, k, :]), scalar=-1.0 / L1_DH, in1=wv[:, k],
                                             op0=ALU.mult, op1=ALU.add).then_inc(once["v_centered"], 1)
                dve.wait_ge(once["bias_b_done"], 2)
                dve.scalar_tensor_tensor(out=bias[:], in0=bias_raw[:], scalar=const2[:, C2_COL:C2_COL + 1], in1=bias_b[:].bitcast(F32),
                                         op0=ALU.mult, op1=ALU.add).then_inc(once["bias_done"], 1)
                for n in range(3):
                    dve.tensor_reduce(t_sum[:, n:n + 1], t_raw[:, parts[n]], AX_X, ALU.add, apply_absolute_value=True).then_inc(once["t_summed"], 1)
                dve.wait_ge(once["t_spread"], 1)
                dve.tensor_scalar(t_thr[:, 0:3], sums[:, 0:3], 1.0 / (FFN * D), 1e-8, ALU.mult, ALU.add).then_inc(once["thr"], 1)
                dve.wait_ge(once["thr"], 1)
                dve.tensor_scalar(t_thr[:, 3:6], t_thr[:, 0:3], -0.5, None, ALU.mult).then_inc(once["thr"], 1)
                dve.wait_ge(once["thr"], 2)
                dve.tensor_scalar(t_thr[:, 0:3], t_thr[:, 0:3], 0.5, None, ALU.mult).then_inc(once["thr"], 1)
                dve.wait_ge(once["thr"], 3)
                for n in range(3):
                    below = below_r[:, 0:parts[n].stop - parts[n].start]
                    dve.tensor_scalar(below, t_raw[:, parts[n]], t_thr[:, 3 + n:4 + n], None, ALU.is_lt).then_inc(once["ternary_step"], 1)
                    dve.wait_ge(once["ternary_step"], n + 1)
                    dve.scalar_tensor_tensor(out=tern[:, parts[n]], in0=t_raw[:, parts[n]], scalar=t_thr[:, n:n + 1],
                                             in1=below, op0=ALU.is_gt, op1=ALU.subtract).then_inc(once["ternary"], 1)
                    dve.wait_ge(once["ternary"], n + 1)


            @block.tensor
            def _(pe):
                pe.wait_ge(once["t_summed"], 3)
                pe.wait_ge(once["zeroed"], 5)
                pe.matmul(sums[:, 0:3], all_ones[:], t_sum[:], start=True, stop=True).then_inc(once["t_spread"], 1)

        xn = sb("l1_xn", [P, 2, KC, P])
        xn_hi = sb("l1_xn_hi", [P, KC, GT], F32R)
        xn_lo = sb("l1_xn_lo", [P, KC, GT], F32R)
        xpad = sb("xpad", [P, KC, BPG, PAD + SEQ])
        cv = sb("cv", [P, KC, GT])
        cs = sb("cs", [P, KC, GT])
        xc_hi = sb("xc_hi", [P, KC, GT], F32R)
        xc_lo = sb("xc_lo", [P, KC, GT], F32R)
        qk = sb("qk", [P, TPG, 2 * D])
        sq = sb("sq", [P, 2, 3 * D])
        ss = sb("ss", [P, TPG, 48])
        vn = sb("vn", [P, TPG, D])
        gates = sb("gates", [P, TPG, 2 * D])
        decay = sb("decay", [P, KC, GT])
        mem = sb("mem", [P, KC, GT])
        sm = sb("sm", [P, TPG, L1_HEADS])
        so = sb("so", [P, TPG, L1_HEADS])
        s2 = sb("s2", [P, TPG, L1_HEADS])
        o = sb("o", [P, TPG, D])
        o_hi = sb("o_hi", [P, 2, KC, P], F32R)
        o_lo = sb("o_lo", [P, 2, KC, P], F32R)
        sig = sb("sig", [P, GT])
        hid = sb("l1_hid", [P, GT])
        h_hi = sb("h_hi", [P, FFN_CHUNKS, GT], F32R)
        h_lo = sb("h_lo", [P, FFN_CHUNKS, GT], F32R)
        res = sb("res", [P, 2, D])

        banks = [ctx.enter_context(nc.psum_tensor(f"lbank{n}", [P, 512], F32)) for n in range(8)]
        PER = dict(xn_ready=TPG, xn_turned=TPG, xn_hi_done=TPG, xpad_done=TPG,
                   xn_lo_done=TPG, conv_step=8, conv_sig=KC, xc_done=KC, xc_hi_done=KC, xc_lo_done=KC,
                   qk_done=TPG, v_done=TPG, qk_copied=TPG, sq_done=TPG, ss_summed=TPG, ss_done=TPG, norm_done=TPG, vn_done=TPG,
                   gamma_done=KC, decay_done=KC, io_done=TPG, gates_done=TPG, kv_done=TPG, b_done=TPG, b_turned=BPG,
                   scan_done=BPG, mem_centered=TPG, mem_sq=TPG, sm_done=TPG, rm_done=TPG, mn_done=TPG, op_done=TPG,
                   so_done=TPG, cen_done=TPG, cen_sq=TPG, s2_done=TPG, ro_done=TPG, on_done=TPG, o_done=TPG,
                   o_turned=TPG, o_hi_done=TPG, o_lo_done=TPG, up_done=FFN_CHUNKS, sig_done=FFN_CHUNKS,
                   hid_done=FFN_CHUNKS, h_hi_done=FFN_CHUNKS, h_lo_done=FFN_CHUNKS, y_done=TPG, res_done=TPG,
                   stored0=8 * TPG, stored1=8 * TPG, chain=TPG * 13)
        S = {n: ctx.enter_context(nc.semaphore(f"l_{n}")) for n in PER}
        prime(nc, list(S.values()))
        pad_zeroed = ctx.enter_context(nc.semaphore("pad_zeroed"))
        block = ctx.enter_context(nc.Block())
        counted = dict.fromkeys(PER, 0)

        def inc(ins, name, by=1):
            counted[name] += by
            ins.then_inc(S[name], by)

        def tile_x(i, t):
            return X[:, bass.ds(i * TPG + t, 1), :].rearrange("p a d -> p (a d)")

        def heads(ap):
            return ap.rearrange("p (h d) -> p h d", d=L1_DH)

        def each(ap, n=L1_HEADS):
            return ap.rearrange("p (h a) -> p h a", a=1).to_broadcast([P, n, L1_DH])

        @block.sync
        def _(sp):
            with sp.Fori(0, GROUPS) as i:
                at = sp.snap(i * GT)
                for t in range(TPG):
                    sp.wait_ge(S["res_done"], START + i * PER["res_done"] + t + 1)
                    inc(sp.dma_start(out[bass.ds(at + P * t, P), :], res[:, t % 2, :]), f"stored{t % 2}", 16)
            for n in range(2):
                sp.wait_ge(S[f"stored{n}"], START + 8 * TILES)

        @block.gpsimd
        def _(pool):
            pool.memset(xpad[:], 0.0).then_inc(pad_zeroed, 1)

            with pool.Fori(0, GROUPS) as i:
                def wait(name, k):
                    pool.wait_ge(S[name], START + i * PER[name] + k)

                links = [0]

                def link(ins):
                    links[0] += 1
                    inc(ins, "chain")
                    wait("chain", links[0])

                for t in range(TPG):
                    wait("ss_done", t + 1)
                    link(pool.tensor_tensor(ss[:, t, :], ss[:, t, :], eps16[:], ALU.add))
                    inc(pool.tensor_tensor(ss[:, t, :], ss[:, t, :], half[:], ALU.pow), "norm_done")
                for k in range(KC):
                    wait("conv_sig", k + 1)
                    inc(pool.tensor_tensor(cs[:, k, :], cv[:, k, :], cs[:, k, :], ALU.mult), "xc_done")
                for k in range(KC):
                    wait("xc_hi_done", k + 1)
                    inc(pool.tensor_tensor(xc_lo[:, k, :], cs[:, k, :], xc_hi[:, k, :].bitcast(F32), ALU.subtract), "xc_lo_done")
                for t in range(TPG):
                    wait("vn_done", t + 1)
                    wait("norm_done", t + 1)
                    wait("qk_copied", t + 1)
                    v, k = vn[:, t, :], qk[:, t, D:2 * D]
                    link(pool.tensor_tensor(heads(v), heads(v), vn_g, ALU.mult))
                    link(pool.tensor_tensor(heads(v), heads(v), vn_b, ALU.add))
                    link(pool.tensor_tensor(heads(k), heads(k), each(ss[:, t, 16:32]), ALU.mult))
                    inc(pool.tensor_tensor(k, k, v, ALU.mult), "kv_done")
                for t in range(TPG):
                    wait("sm_done", t + 1)
                    link(pool.tensor_tensor(sm[:, t, :], sm[:, t, :], eps16[:, 32:48], ALU.add))
                    inc(pool.tensor_tensor(sm[:, t, :], sm[:, t, :], half[:, 0:16], ALU.pow), "rm_done")
                for t in range(TPG):
                    wait("mn_done", t + 1)
                    link(pool.tensor_tensor(heads(o[:, t, :]), heads(o[:, t, :]), mn_g, ALU.mult))
                    link(pool.tensor_tensor(heads(o[:, t, :]), heads(o[:, t, :]), mn_b, ALU.add))
                    inc(pool.tensor_tensor(o[:, t, :], o[:, t, :], qk[:, t, 0:D], ALU.mult), "op_done")
                for t in range(TPG):
                    wait("s2_done", t + 1)
                    rq = ss[:, t, 0:16]
                    link(pool.tensor_tensor(s2[:, t, :], s2[:, t, :], rq, ALU.mult))
                    link(pool.tensor_tensor(s2[:, t, :], s2[:, t, :], rq, ALU.mult))
                    link(pool.tensor_tensor(s2[:, t, :], s2[:, t, :], eps16[:, 32:48], ALU.add))
                    link(pool.tensor_tensor(s2[:, t, :], s2[:, t, :], half[:, 0:16], ALU.pow))
                    inc(pool.tensor_tensor(s2[:, t, :], s2[:, t, :], rq, ALU.mult), "ro_done")
                for t in range(TPG):
                    wait("on_done", t + 1)
                    link(pool.tensor_tensor(o[:, t, :], o[:, t, :], gn_g, ALU.mult))
                    link(pool.tensor_tensor(o[:, t, :], o[:, t, :], gn_b, ALU.add))
                    inc(pool.tensor_tensor(o[:, t, :], o[:, t, :], gates[:, t, D:2 * D], ALU.mult), "o_done")

        @block.scalar
        def _(act):
            act.wait_ge(pad_zeroed, 1)

            with act.Fori(0, GROUPS) as i:
                def wait(name, k):
                    act.wait_ge(S[name], START + i * PER[name] + k)

                def ffn_act(c):
                    wait("up_done", c + 1)
                    wait("hid_done", c)
                    inc(act.activation(sig[:], banks[6][:], ACT.Sigmoid), "sig_done")
                    wait("hid_done", c + 1)
                    if c == 0:
                        wait("y_done", 0)
                    inc(act.activation(h_hi[:, c, :], hid[:], ACT.Copy), "h_hi_done")

                for t in range(TPG):
                    wait("xn_turned", t + 1)
                    src = banks[t % 2][:, 0:D].rearrange("p (k n) -> p k n", k=KC)
                    if t == 0:
                        wait("gates_done", 0)
                        wait("conv_step", 0)
                        act.wait_ge(S["up_done"], START + i * PER["up_done"])
                    inc(act.activation(xn_hi[:, :, P * t:P * t + P], src, ACT.Copy), "xn_hi_done")
                    inc(act.activation(xpad[:, :, t // 2, PAD + P * (t % 2):PAD + P * (t % 2) + P], src, ACT.Copy), "xpad_done")
                for t in range(TPG):
                    wait("qk_done", t + 1)
                    wait("op_done", 0)
                    inc(act.activation(qk[:, t, :], banks[2 + t % 2][:], ACT.Copy), "qk_copied")
                    wait("v_done", t + 1)
                    if t >= 2:
                        wait("ss_done", t - 1)
                    else:
                        wait("ss_done", 0)
                    act.activation(sq[:, t % 2, 0:2 * D], banks[2 + t % 2][:], ACT.Square)
                    inc(act.activation(sq[:, t % 2, 2 * D:3 * D], banks[4 + t % 2][:, 0:D], ACT.Square), "sq_done")
                for k in range(KC):
                    wait("conv_step", 7 + k)
                    wait("xc_lo_done", 0)
                    inc(act.activation(cs[:, k, :], cv[:, k, :], ACT.Sigmoid), "conv_sig")
                for k in range(KC):
                    wait("xc_done", k + 1)
                    if k == 0:
                        wait("io_done", 0)
                    inc(act.activation(xc_hi[:, k, :], cs[:, k, :], ACT.Copy), "xc_hi_done")
                ffn_act(0)
                ffn_act(1)
                for m in range(KC):
                    wait("gamma_done", m + 1)
                    wait("scan_done", 0)
                    inc(act.activation(decay[:, m, :], banks[m][:], ACT.Sigmoid, bias=gamma_b[:, m:m + 1]), "decay_done")
                for t in range(TPG):
                    wait("io_done", t + 1)
                    wait("o_done", 0)
                    inc(act.activation(gates[:, t, :], banks[2 + t % 2][:], ACT.Sigmoid), "gates_done")
                ffn_act(2)
                ffn_act(3)
                for t in range(TPG):
                    wait("mem_centered", t + 1)
                    if t >= 2:
                        wait("sm_done", t - 1)
                    inc(act.activation(sq[:, t % 2, 0:D], banks[t % 2][:, 0:D], ACT.Square), "mem_sq")
                ffn_act(4)
                ffn_act(5)
                for t in range(TPG):
                    wait("cen_done", t + 1)
                    if t >= 2:
                        wait("s2_done", t - 1)
                    else:
                        wait("sm_done", TPG)
                    inc(act.activation(sq[:, t % 2, 0:D], o[:, t, :], ACT.Square), "cen_sq")
                for t in range(TPG):
                    wait("o_turned", t + 1)
                    if t >= 2:
                        wait("y_done", t - 1)
                    else:
                        wait("y_done", 0)
                    inc(act.activation(o_hi[:, t % 2, :, :], banks[2 + t % 2][:, 0:D].rearrange("p (k n) -> p k n", k=KC), ACT.Copy), "o_hi_done")

        @block.vector
        def _(dve):
            with dve.Fori(0, GROUPS) as i:
                def wait(name, k):
                    dve.wait_ge(S[name], START + i * PER[name] + k)

                def ffn_dve(c):
                    wait("sig_done", c + 1)
                    if c == 0:
                        wait("h_lo_done", 0)
                    inc(dve.tensor_tensor(hid[:], sig[:], banks[7][:], ALU.mult), "hid_done")
                    wait("h_hi_done", c + 1)
                    inc(dve.tensor_tensor(h_lo[:, c, :], hid[:], h_hi[:, c, :].bitcast(F32), ALU.subtract), "h_lo_done")
                    wait("h_lo_done", c + 1)

                def normalise(t):
                    if t >= 2:
                        wait("xn_turned", t - 1)
                    else:
                        wait("xn_turned", 0)
                    inc(dve.tensor_scalar(xn[:, t % 2, :, :], tile_x(i, t).rearrange("p (j k) -> p k j", k=KC), mv[:, bass.ds(i * TPG + t, 1), 0],
                                          rstd[:, bass.ds(i * TPG + t, 1)], ALU.subtract, ALU.mult), "xn_ready")

                normalise(0)
                for t in range(TPG):
                    if t + 1 < TPG:
                        normalise(t + 1)
                    wait("xpad_done", t + 1)
                    inc(dve.tensor_tensor(xn_lo[:, :, P * t:P * t + P], banks[t % 2][:, 0:D].rearrange("p (k n) -> p k n", k=KC),
                                          xn_hi[:, :, P * t:P * t + P].bitcast(F32), ALU.subtract), "xn_lo_done")
                wait("xpad_done", TPG)
                wait("xc_done", 0)
                n = 0
                for tap in range(TAPS):
                    for k in range(KC):
                        src = xpad[:, k, :, tap:tap + SEQ]
                        dst = cv[:, k, :].rearrange("p (b s) -> p b s", b=BPG)
                        if tap == 0:
                            ins = dve.tensor_scalar(dst, src, conv[:, k, 0:1], conv[:, k, TAPS:TAPS + 1], ALU.mult, ALU.add)
                        else:
                            wait("conv_step", n - 1)
                            ins = dve.scalar_tensor_tensor(out=dst, in0=src, scalar=conv[:, k, tap:tap + 1], in1=dst, op0=ALU.mult, op1=ALU.add)
                        inc(ins, "conv_step")
                        n += 1
                for t in range(TPG):
                    wait("sq_done", t + 1)
                    if t == 0:
                        wait("ro_done", 0)
                    inc(dve.tensor_reduce(ss[:, t, :], heads(sq[:, t % 2, :]), AX_X, ALU.add), "ss_summed")
                    if t >= 1:
                        values_normed(dve, wait, inc, vn, banks, ss, t - 1, heads, each)
                    wait("ss_summed", t + 1)
                    inc(dve.tensor_scalar(ss[:, t, :], ss[:, t, :], 1e-24, None, ALU.max), "ss_done")
                values_normed(dve, wait, inc, vn, banks, ss, TPG - 1, heads, each)
                ffn_dve(0)
                ffn_dve(1)
                for t in range(TPG):
                    wait("kv_done", t + 1)
                    wait("gates_done", t + 1)
                    inc(dve.tensor_tensor(vn[:, t, :], qk[:, t, D:2 * D], gates[:, t, 0:D], ALU.mult), "b_done")
                ffn_dve(2)
                ffn_dve(3)
                for b in range(BPG):
                    wait("b_turned", b + 1)
                    wait("decay_done", KC)
                    if b == 0:
                        wait("mem_centered", 0)
                    for m in range(KC):
                        ins = dve.tensor_tensor_scan(mem[:, m, SEQ * b:SEQ * b + SEQ], decay[:, m, SEQ * b:SEQ * b + SEQ],
                                                     banks[4 + b][:, SEQ * m:SEQ * m + SEQ], 0.0, ALU.mult, ALU.add)
                    inc(ins, "scan_done")
                for t in range(TPG):
                    wait("mem_sq", t + 1)
                    inc(dve.tensor_reduce(sm[:, t, :], heads(sq[:, t % 2, 0:D]), AX_X, ALU.add), "sm_done")
                    if t >= 1:
                        memory_normed(dve, wait, inc, o, banks, sm, t - 1, heads, each)
                memory_normed(dve, wait, inc, o, banks, sm, TPG - 1, heads, each)
                ffn_dve(4)
                ffn_dve(5)
                for t in range(TPG):
                    wait("op_done", t + 1)
                    inc(dve.tensor_reduce(so[:, t, :], heads(o[:, t, :]), AX_X, ALU.add), "so_done")
                    wait("so_done", t + 1)
                    inc(dve.scalar_tensor_tensor(out=heads(o[:, t, :]), in0=each(so[:, t, :]), scalar=-1.0 / L1_DH, in1=heads(o[:, t, :]),
                                                 op0=ALU.mult, op1=ALU.add), "cen_done")
                for t in range(TPG):
                    wait("cen_sq", t + 1)
                    inc(dve.tensor_reduce(s2[:, t, :], heads(sq[:, t % 2, 0:D]), AX_X, ALU.add), "s2_done")
                for t in range(TPG):
                    wait("ro_done", t + 1)
                    inc(dve.tensor_tensor(heads(o[:, t, :]), heads(o[:, t, :]), each(s2[:, t, :]), ALU.mult), "on_done")
                for t in range(TPG):
                    wait("o_hi_done", t + 1)
                    inc(dve.tensor_tensor(o_lo[:, t % 2, :, :], banks[2 + t % 2][:, 0:D].rearrange("p (k n) -> p k n", k=KC),
                                          o_hi[:, t % 2, :, :].bitcast(F32), ALU.subtract), "o_lo_done")
                    if t >= 1:
                        residual(dve, wait, inc, res, banks, tile_x(i, t - 1), t - 1)
                residual(dve, wait, inc, res, banks, tile_x(i, TPG - 1), TPG - 1)

        @block.tensor
        def _(pe):
            with pe.Fori(0, GROUPS) as i:
                def wait(name, k):
                    pe.wait_ge(S[name], START + i * PER[name] + k)

                def product(dst, lhs, rhs, first=True, last=True):
                    n = 0
                    for a, b in ((0, 0), (0, 1), (1, 0)):
                        for k in range(KC):
                            mm = pe.matmul(dst, lhs[a](k), rhs[b](k), start=(first and n == 0), stop=(last and n == 3 * KC - 1))
                            n += 1
                    return mm

                def rows(hi, lo, t):
                    return [lambda k, x=x: x[:, k, P * t:P * t + P] for x in (hi, lo)]

                def cols(a, b):
                    return [lambda k, x=x: x[:, k, a:b] for x in (w_hi, w_lo)]

                def ffn_up(c):
                    wait("hid_done", c)
                    for bank, w in ((6, w1), (7, w2)):
                        n = 0
                        for x in (xn_hi, xn_lo):
                            for k in range(KC):
                                mm = pe.matmul(banks[bank][:], w[:, k, P * c:P * c + P], x[:, k, :], start=(n == 0), stop=(n == 3))
                                n += 1
                    inc(mm, "up_done")

                for t in range(TPG):
                    wait("xn_ready", t + 1)
                    if t >= 2:
                        wait("xn_lo_done", t - 1)
                        wait("xpad_done", t - 1)
                    elif t == 0:
                        wait("mn_done", 0)
                    for k in range(KC):
                        mm = pe.transpose(banks[t % 2][:, P * k:P * k + P], xn[:, t % 2, k, :], ident[:])
                    inc(mm, "xn_turned")
                wait("o_lo_done", 0)
                wait("res_done", 0)
                for t in range(TPG):
                    if t < 2:
                        wait("xn_lo_done", TPG)
                    if t >= 2:
                        wait("sq_done", t - 1)
                        wait("qk_copied", t - 1)
                    inc(product(banks[2 + t % 2][:], rows(xn_hi, xn_lo, t), cols(W_QK, W_V)), "qk_done")
                    if t >= 2:
                        wait("vn_done", t - 1)
                    inc(product(banks[4 + t % 2][:, 0:D], rows(xn_hi, xn_lo, t), cols(W_V, W_IO)), "v_done")
                ffn_up(0)
                ffn_up(1)
                wait("xc_lo_done", KC)
                wait("xn_lo_done", TPG)
                wait("xpad_done", TPG)
                for m in range(KC):
                    inc(product(banks[m][:], cols(W_G + P * m, W_G + P * m + P), [lambda k, x=x: x[:, k, :] for x in (xc_hi, xc_lo)]), "gamma_done")
                for t in range(TPG):
                    if t < 2:
                        wait("sq_done", TPG)
                        wait("qk_copied", TPG)
                    else:
                        wait("gates_done", t - 1)
                    bank = banks[2 + t % 2][:]
                    product(bank, rows(xc_hi, xc_lo, t), cols(W_IO, W_G), last=False)
                    inc(pe.matmul(bank, ones_rows[:], bias[:], start=False, stop=True), "io_done")
                ffn_up(2)
                ffn_up(3)
                wait("vn_done", TPG)
                for t in range(TPG):
                    wait("b_done", t + 1)
                    for m in range(KC):
                        mm = pe.transpose(banks[4 + t // 2][:, SEQ * m + P * (t % 2):SEQ * m + P * (t % 2) + P], vn[:, t, P * m:P * m + P], ident[:])
                    if t % 2:
                        inc(mm, "b_turned")
                wait("decay_done", KC)
                for t in range(TPG):
                    wait("scan_done", t // 2 + 1)
                    if t >= 2:
                        wait("mn_done", t - 1)
                    for m in range(KC):
                        mm = pe.matmul(banks[t % 2][:, P * m:P * m + P], mem[:, m, P * t:P * t + P], center, start=True, stop=True)
                    inc(mm, "mem_centered")
                ffn_up(4)
                ffn_up(5)
                wait("gates_done", TPG)
                for t in range(TPG):
                    wait("o_done", t + 1)
                    if t >= 2:
                        wait("o_lo_done", t - 1)
                    for m in range(KC):
                        mm = pe.transpose(banks[2 + t % 2][:, P * m:P * m + P], o[:, t, P * m:P * m + P], ident[:])
                    inc(mm, "o_turned")
                    if t >= 1:
                        output(pe, wait, inc, product, banks, t - 1, o_hi, o_lo, wo_hi, wo_lo, h_hi, h_lo, w3)
                output(pe, wait, inc, product, banks, TPG - 1, o_hi, o_lo, wo_hi, wo_lo, h_hi, h_lo, w3)

        assert counted == PER


N_LOADS = 16


def values_normed(dve, wait, inc, vn, banks, ss, t, heads, each):
    wait("norm_done", t + 1)
    if t == 0:
        wait("b_turned", 0)
    inc(dve.tensor_tensor(heads(vn[:, t, :]), heads(banks[4 + t % 2][:, 0:D]), each(ss[:, t, 32:48]), ALU.mult), "vn_done")


def memory_normed(dve, wait, inc, o, banks, sm, t, heads, each):
    wait("rm_done", t + 1)
    if t == 0:
        wait("o_turned", 0)
    inc(dve.tensor_tensor(heads(o[:, t, :]), heads(banks[t % 2][:, 0:D]), each(sm[:, t, :]), ALU.mult), "mn_done")


def residual(dve, wait, inc, res, banks, xt, t):
    wait("y_done", t + 1)
    wait(f"stored{t % 2}", 16 * (t // 2))
    inc(dve.tensor_tensor(res[:, t % 2, :], banks[4 + t % 2][:, 0:D], xt, ALU.add), "res_done")


def output(pe, wait, inc, product, banks, t, o_hi, o_lo, wo_hi, wo_lo, h_hi, h_lo, w3):
    wait("o_lo_done", t + 1)
    wait("h_lo_done", FFN_CHUNKS)
    wait("scan_done", BPG)
    if t >= 2:
        wait("res_done", t - 1)
    dst = banks[4 + t % 2][:, 0:D]
    product(dst, [lambda k, x=x: x[:, t % 2, k, :] for x in (o_hi, o_lo)], [lambda k, x=x: x[:, k, :] for x in (wo_hi, wo_lo)], last=False)
    for n, h in enumerate((h_hi, h_lo)):
        for c in range(FFN_CHUNKS):
            mm = pe.matmul(dst, h[:, c, P * t:P * t + P], w3[:, c, :], start=False, stop=(n == 1 and c == FFN_CHUNKS - 1))
    inc(mm, "y_done")


def build(nc, dram, out):
    with ExitStack() as stack:
        def sb(name, shape, dt=F32):
            return stack.enter_context(nc.sbuf_tensor(name, shape, dt))

        keep = {
            "X": sb("X", [P, TILES, D]),
            "ident": sb("ident", [P, P]),
            "eps": sb("eps", [P, 1]),
        }
        start = stack.enter_context(nc.semaphore("start"))
        with nc.Block() as block:
            @block.vector
            def _(dve):
                dve.memset(keep["eps"][:], EPS).then_inc(start, 1)
        with (
            nc.sbuf_tensor("xall_hi", [P, KC, TOK], F32R) as keep["xall_hi"],
            nc.sbuf_tensor("xall_lo", [P, KC, TOK], F32R) as keep["xall_lo"],
        ):
            layer0_attention(nc, stack, dram, keep)
            layer0_mlp(nc, dram, keep)
        layer1(nc, dram, keep, out)


def layouts(inputs, np):
    f = {k: np.asarray(v) for k, v in inputs.items()}
    a = {"x": f["L0_attn_x"].reshape(TOK, D)}

    def turned(w):
        return np.ascontiguousarray(w.T).reshape(P, KC, w.shape[0])

    wk = f["L0_attn_Wk"]
    a["wqkv"] = np.concatenate([turned(f["L0_attn_Wq"]), turned(wk), turned(wk), turned(f["L0_attn_Wv"])], axis=2)
    a["memory"] = f["L0_attn_memory"]
    a["memory_norm"] = f["L0_attn_memory_norm"]
    a["memory_weight"] = f["L0_attn_memory_weight"]
    c = np.zeros((P, NCONST), np.float32)
    c[:, C_ID:C_ID + P] = np.eye(P)
    for quad in range(2):
        for j in range(2):
            for hq in range(4):
                for d in range(DH):
                    src = 64 * j + (4 * quad + hq) * DH + d
                    v = 2 * (2 * quad + j)
                    for r, part in ((0, 0), (1, 1), (2, 0)):
                        c[src, C_SELQ + (v + part) * P + 3 * DH * hq + DH * r + d] = 1.0
    for h in range(HEADS):
        for d in range(DH):
            for r, part in ((0, 0), (1, 0), (2, 1)):
                c[64 * part + h * DH + d, C_SELK + h * P + 3 * DH * (h % 4) + DH * r + d] = 1.0
    c[64:, C_COL] = 1.0
    c[:64, C_COL + 1] = 1.0
    c[64:, C_COL + 1] = -1.0
    for hq in range(4):
        c[ROWS + 2 * hq:ROWS + 2 * hq + 2, C_COL + 2 + hq] = 1.0
    a["const"] = c

    def by_chunk(g):
        return g.reshape(PAIRS_N, P, 2, -1).transpose(3, 0, 2, 1).reshape(-1, PAIRS_N, D)

    gate, up = by_chunk(f["L0_ffn_gate_W_packed"]), by_chunk(f["L0_ffn_up_W_packed"])
    down = f["L0_ffn_down_W_packed"].T.reshape(PAIRS_N, P, D).transpose(1, 0, 2)
    a["codes"] = np.concatenate([gate, up, down], axis=2)
    rows = 2 * P // NVFP_BLOCK
    s_gate, s_up = by_chunk(f["L0_ffn_gate_scales"]), by_chunk(f["L0_ffn_up_scales"])
    s_down = f["L0_ffn_down_scales"].T.reshape(PAIRS_N, rows, D).transpose(1, 0, 2)
    a["scales"] = np.repeat(np.concatenate([s_gate, s_up, s_down], axis=2), P // rows, axis=0)

    l1 = {k[3:]: v for k, v in f.items() if k.startswith("L1_")}
    gamma_w = np.repeat(l1["attn_gamma_w"], L1_DH, axis=0)
    a["l1w"] = np.concatenate([turned(w) for w in (l1["attn_Wq"], l1["attn_Wk"], l1["attn_Wv"], l1["attn_ig_w"], l1["attn_og_w"], gamma_w)], axis=2)
    a["wo"] = l1["attn_Wo"].T.reshape(KC, P, D).transpose(1, 0, 2)
    a["conv"] = np.concatenate([l1["attn_conv_w"][:, 0, :].reshape(P, KC, TAPS), l1["attn_conv_b"].reshape(P, KC, 1)], axis=2)
    a["gamma_b"] = np.repeat(l1["attn_gamma_b"], L1_DH).reshape(KC, P).T
    for name in ("vn_g", "vn_b", "mn_g", "mn_b", "gn_g", "gn_b", "ig_b", "og_b"):
        a[name] = l1["attn_" + name]
    wide = FFN_CHUNKS * P
    up = [np.concatenate([turned(l1[n]), np.zeros((P, KC, wide - FFN), np.float32)], axis=2).reshape(P, -1) for n in ("ffn_w1", "ffn_w2")]
    w3 = np.concatenate([l1["ffn_w3"].T, np.zeros((wide - FFN, D), np.float32)], axis=0)
    a["ternary"] = np.concatenate(up + [w3.reshape(FFN_CHUNKS, P, D).transpose(1, 0, 2).reshape(P, -1)], axis=1)
    c = np.zeros((P, N_CONST2), np.float32)
    c[0:2, C2_E:C2_E + P] = 1.0
    c[:, C2_CENTER:C2_CENTER + P] = np.eye(P) - np.kron(np.eye(P // L1_DH), np.full((L1_DH, L1_DH), 1.0 / L1_DH))
    c[1, C2_COL] = 1.0
    c[0, C2_COL + 1] = 1.0
    c[1, C2_COL + 1] = -1.0
    a["const2"] = c
    return a


def kernel(**inputs):
    import numpy as np
    import concourse.bacc as bacc
    from concourse.bass_utils import run_bass_kernel_spmd

    nc = bacc.Bacc("TRN2", target_bir_lowering=False, num_devices=1)
    arrays, dram = {}, {}
    for name, a in layouts(inputs, np).items():
        a = np.ascontiguousarray(a)
        arrays[f"in_{name}"] = a
        dram[name] = nc.dram_tensor(f"in_{name}", a.shape, mybir.dt.from_np(a.dtype), kind="ExternalInput").ap()
    out = nc.dram_tensor("out", (TOK, D), F32, kind="ExternalOutput").ap()
    build(nc, dram, out)
    r = run_bass_kernel_spmd(nc, [arrays], core_ids=[0])
    return r.results[0]["out"].reshape(BATCH, SEQ, D)
```

```python
from contextlib import ExitStack

import concourse.bass as bass
from concourse import mybir

ALU = mybir.AluOpType
ACT = mybir.ActivationFunctionType
AX_X = mybir.AxisListType.X
F32 = mybir.dt.float32
F32R = mybir.dt.float32r
I32 = mybir.dt.int32
U16 = mybir.dt.uint16
BF16 = mybir.dt.bfloat16
F8 = mybir.dt.float8e4

P = 128
D = 256
KC = D // P
BATCH, SEQ = 8, 256
TOK = BATCH * SEQ
TILES = TOK // P
GROUPS = 4
GT = TOK // GROUPS
TPG = GT // P
BPG = BATCH // GROUPS
EPS = 1e-5

HEADS, QPK, DH = 8, 4, 8
DKV = HEADS * DH
SCALE = float(DH) ** -0.5
UNITS = BPG * HEADS
QKV = D + P + DKV
ROWS = 4 * 3 * DH
C_ID, C_SELQ, C_SELK, C_COL = 0, P, P + 8 * P, P + 16 * P
NCONST = C_COL + 6

START = 40
IN_LOOPS_1 = """down_step gate_done gelu_done hid_done hid_hi_done hid_lo_done up_done x_updated y_done y_turned stats_done""".split()


def prime(sp, semaphores):
    for s in semaphores:
        sp.sem_inc(s, START)


SLOTS = 19
SCHEDULE = {
    2: [('normalise', 0)],
    3: [('turn', 0), ('normalise', 1)],
    4: [('turn', 1), ('q', 0)],
    5: [('q', 1)],
    6: [('reciprocal', 0), ('k', 0)],
    7: [('selk', 0), ('reciprocal', 1)],
    8: [('selk', 1)],
    9: [('selq', 0), ('selq', 1)],
    10: [('selk', 2), ('selq', 2)],
    11: [('selk', 3), ('selq', 3)],
    12: [('selk', 4), ('memory', 0)],
    13: [('memory', 1), ('selk', 5)],
    14: [('selk', 6), ('memory', 2)],
    15: [('memory', 3)],
    16: [('v', 0)],
}
SELECT_LATE = {0: [('selq', 4)], 1: [('selk', 7), ('selq', 5), ('selq', 6)], 2: [('selq', 7)]}
PREP_ORDER = [s for slot in sorted(SCHEDULE) for s in SCHEDULE[slot] if s[0] not in ("normalise", "reciprocal")]
PREP_ORDER += [s for slot in sorted(SELECT_LATE) for s in SELECT_LATE[slot]]
SELECTIONS = [s for s in PREP_ORDER if s[0] in ("selk", "selq")]
SEL_ACT = [s for s in SELECTIONS if s not in [('selq', 0), ('selq', 7), ('selq', 1)]]
SEL_DVE = [s for s in SELECTIONS if s not in SEL_ACT]
DECODE_AT = [11, 15]


def layer0_attention(nc, dram, keep):
    X, ident = keep["X"], keep["ident"]
    with ExitStack() as ctx:
        def sb(name, shape, dt=F32):
            return ctx.enter_context(nc.sbuf_tensor(name, shape, dt))

        def sem(name):
            return ctx.enter_context(nc.semaphore(name))

        const = sb("const", [P, NCONST])
        sel_q = sb("sel_q", [P, 8, P], F32R)
        sel_k = sb("sel_k", [P, 8, P], F32R)
        alpha, beta = const[:, C_COL:C_COL + 1], const[:, C_COL + 1:C_COL + 2]
        w_raw = sb("w_raw", [P, KC, QKV])
        w_hi = sb("w_hi", [P, KC, QKV], F32R)
        w_lo = sb("w_lo", [P, KC, QKV], F32R)
        mem2 = sb("mem2", [P, 2, DKV + 1])
        mw = sb("mw", [P, 4])
        stats = keep["stats"]
        mv = sb("mv", [P, TILES, 2])
        rstd = sb("rstd", [P, TILES])
        xn = sb("xn", [P, 2, KC, P])
        xn_hi = sb("xn_hi", [P, KC, GT], F32R)
        xn_lo = sb("xn_lo", [P, KC, GT], F32R)
        q_hi = sb("q_hi", [P, 2, GT], F32R)
        q_lo = sb("q_lo", [P, 2, GT], F32R)
        q_neg, q_rec, sigma = (keep["shared"][:, 2 * GT * n:2 * GT * n + 2 * GT].rearrange("p (c n) -> p c n", c=2) for n in range(3))
        codes = [w_raw[:].rearrange("p k n -> p (k n)")[:, 0:WORDS].bitcast(I32), sb("codes", [P, WORDS], I32)[:]]
        k_b = sb("k_b", [P, GT], F32R)
        k_parts = sb("k_parts", [P, GT], F32R)
        Q = sb("Q", [P, 2, BPG, QPK, SEQ], F32R)
        K = sb("K", [P, HEADS, GT], F32R)
        V = sb("V", [P, TPG, HEADS, 32])
        neg_max = sb("neg_max", [P, 2, 8])
        max_parts = sb("max_parts", [8, 2, 2, P], F32R)
        probs = sb("probs", [P, 4, 2, 2, 512])
        o_sb = sb("o_sb", [P, 2, 512])
        o_rec = sb("o_rec", [P, 16])
        att = sb("att", [P, TPG, D])
        a_rec = sb("a_rec", [P, 4])
        a_mem = sb("a_mem", [P, D])
        code_part = sb("code_part", [P, WORDS], I32)

        banks = [ctx.enter_context(nc.psum_tensor(f"bank{n}", [P, 512], F32)) for n in range(8)]
        PREP = banks[5]

        names = "loaded xloaded0 xloaded1 xloaded2 xloaded3 const_ready zeroed stats_done w_ready mv_ready std_ready rstd_ready mw_ready".split()
        NS, PAIRS = 4 * UNITS, UNITS // 2
        PER = dict(codes_loaded=32, decoded=10, xn_ready=TPG, xn_turned=2, xn_hi_done=2, xn_lo_done=2, xn_saved=32,
                   q_done=2, q_hi_done=2, q_tanh_done=2, q_lo_done=2, q_relu_done=2, q_neg_done=2, q_rec_step=2, q_rec_done=2,
                   sigma_step=2, sigma_done=2, k_done=1, k_b_done=1, k_parts_done=1, v_proj=1, v_done=1,
                   selected=16, sel_act=len(SEL_ACT), sel_dve=len(SEL_DVE), mem_mm=TPG, mem_done=3 * TPG,
                   s_done=NS, max_done=NS, max_turned=UNITS, max_hi_done=UNITS, max_split=UNITS, max_placed=32 * UNITS,
                   st_done=NS, probs_done=NS, pv_done=PAIRS, pv_copied=PAIRS, o_turned=PAIRS, o_normed=5 * PAIRS, x_updated=1)
        S = {n: sem(f"a_{n}") for n in names + list(PER)}
        block = ctx.enter_context(nc.Block())
        counted = dict.fromkeys(PER, 0)

        def inc(ins, name, by=1):
            counted[name] += by
            ins.then_inc(S[name], by)

        def waiter(engine, g):
            def wait(name, k):
                engine.wait_ge(S[name], START + g * PER[name] + k)
            return wait

        def tile(g, t, n=1):
            at = g * TPG + t
            return slice(at, at + n) if isinstance(g, int) else bass.ds(at, n)

        def prep_bank(other, kind, n):
            at = PREP_ORDER.index((kind, n)) - PREP_ORDER.index(("k", 0))
            return banks[(5, 4, 7)[at % 3]] if other is None and at > 0 else banks[5]

        def selections_done(wait, steps):
            for name, order in (("sel_act", SEL_ACT), ("sel_dve", SEL_DVE)):
                k = max((order.index(s) + 1 for s in steps if s in order), default=0)
                if k:
                    wait(name, k)

        def run_turns(engine, unit, step):
            def turn(late, early):
                if late is None:
                    for slot in range(SLOTS):
                        for kind, n in SCHEDULE.get(slot, []):
                            step(early, None, kind, n)
                    for slot in (-2, -1):
                        unit(early, slot, lambda half: None)
                    return
                for slot in range(SLOTS):
                    def between(half):
                        own, prepared = SELECT_LATE.get(slot, []), SCHEDULE.get(slot, [])
                        both = [(late, late - 1, *s) for s in own] + ([(early, late, *s) for s in prepared] if early is not None else [])
                        for s in (both[0:1], both[1:])[half]:
                            step(*s)
                    unit(late, slot, between)
                    if UNITS <= slot < UNITS + 2 and early is not None:
                        unit(early, slot - UNITS - 2, lambda half: None)

            before = dict(counted)
            turn(None, 0)
            counted.update(before)
            with engine.Fori(0, GROUPS - 1) as i:
                turn(i, i + 1)
            whole = dict(counted)
            turn(GROUPS - 1, None)
            counted.update(whole)

        def select(engine, g, other, kind, n):
            wait = waiter(engine, g)
            bank = prep_bank(other, kind, n)
            wait("selected", SELECTIONS.index((kind, n)) + 1)
            if kind == "selk":
                if other is not None:
                    waiter(engine, other)("st_done", 8 * n + 8)
                inc(engine.activation(K[:, n, :], bank[:], ACT.Identity, bias=const[:, C_COL + 2 + n % 4:C_COL + 3 + n % 4]), "sel_act")
                return
            if other is not None:
                waiter(engine, other)("st_done", NS // 2 * (n // QPK + 1))
            dst, src = Q[:, n // QPK, :, n % QPK, :], bank[:].rearrange("p (b s) -> p b s", b=BPG)
            if (kind, n) in SEL_ACT:
                inc(engine.activation(dst, src, ACT.Copy), "sel_act")
            else:
                inc(engine.tensor_copy(dst, src), "sel_dve")

        @block.sync
        def _(sp):
            def load_rows(n):
                rows = slice(GT * n, GT * n + GT)
                sp.dma_start(X[:, TPG * n:TPG * n + TPG, :], dram["x"][rows, :].rearrange("(n p) d -> p n d", p=P)).then_inc(S[f"xloaded{n}"], 16)

            load_rows(0)
            sp.dma_start(const[:], dram["const"]).then_inc(S["loaded"], 16)
            sp.dma_start(w_raw[:], dram["wqkv"]).then_inc(S["loaded"], 16)
            sp.wait_ge(S["zeroed"], 2)
            for j in range(2):
                sp.dma_start(mem2[64 * j:64 * j + 64, j, 0:DKV], dram["memory"]).then_inc(S["loaded"], 16)
                sp.dma_start(mem2[64 * j:64 * j + 64, j, DKV:DKV + 1], dram["memory_norm"]).then_inc(S["loaded"], 16)
            sp.dma_start(mw[:, 0:1], dram["memory_weight"].rearrange("(a b) -> a b", a=1).partition_broadcast(P)).then_inc(S["loaded"], 16)
            for n in range(1, GROUPS):
                load_rows(n)
            prime(sp, [S[n] for n in PER])
            sp.wait_ge(S["w_ready"], 1)

            def save(g, at):
                wait = waiter(sp, g)
                wait("xn_lo_done", 2)
                for name, part in (("xall_hi", xn_hi), ("xall_lo", xn_lo)):
                    inc(sp.dma_start(keep[name][:, :, at].bitcast(F32), part[:].bitcast(F32)), "xn_saved", 16)

            def turn(late, early):
                if early is not None:
                    at_early = bass.ds(sp.snap(early * GT), GT) if late is not None else slice(0, GT)
                if late is not None:
                    wait = waiter(sp, late)
                    wait("decoded", 0)
                    for n in range(2):
                        pair = late * 2 + n
                        pair = slice(pair, pair + 1) if isinstance(late, int) else bass.ds(pair, 1)
                        inc(sp.dma_start(codes[n], dram["codes"][:, pair, :].rearrange("p a n -> p (a n)")), "codes_loaded", 16)
                    for u in range(UNITS):
                        h, b = divmod(u, BPG)
                        row = ROWS + 2 * (h % 4)
                        wait("max_split", u + 1)
                        for part in range(2):
                            inc(sp.dma_start(
                                Q[row + part:row + part + 1, h // 4, b, :, :].rearrange("a q (s n) -> a (q s) n", n=P).bitcast(F32),
                                max_parts[:, u % 2, part, :].bitcast(F32)), "max_placed", 16)
                        if u == 5 and early is not None:
                            save(early, at_early)
                elif early is not None:
                    save(early, at_early)

            before = dict(counted)
            turn(None, 0)
            counted.update(before)
            with sp.Fori(0, GROUPS - 1) as i:
                turn(i, i + 1)
            whole = dict(counted)
            turn(GROUPS - 1, None)
            counted.update(whole)
            sp.wait_ge(S["xn_saved"], START + 32 * GROUPS)

        @block.gpsimd
        def _(pool):
            pool.memset(keep["eps"][:], EPS).then_inc(S["zeroed"], 1)
            pool.memset(mem2[:], 0.0).then_inc(S["zeroed"], 1)
            pool.memset(V[:], 0.0).then_inc(S["zeroed"], 1)
            pool.wait_ge(S["zeroed"], 3)
            pool.memset(V[:, :, :, DH:DH + 1], 1.0).then_inc(S["zeroed"], 1)
            with pool.Fori(0, GROUPS) as i:
                wait = waiter(pool, i)
                for c in range(2):
                    wait("q_rec_done", c + 1)
                    wait("q_relu_done", c + 1)
                    inc(pool.tensor_tensor(q_neg[:, c, :], q_neg[:, c, :], q_rec[:, c, :], ALU.mult), "sigma_step")
                    wait("sigma_step", c + 1)
                    inc(pool.tensor_tensor(sigma[:, c, :], sigma[:, c, :], q_neg[:, c, :], ALU.subtract), "sigma_done")

        @block.scalar
        def _(act):
            act.wait_ge(S["loaded"], 16 * 7)
            act.activation(ident[:], const[:, C_ID:C_ID + P], ACT.Copy).then_inc(S["const_ready"], 1)
            act.activation(sel_q[:].rearrange("p a b -> p (a b)"), const[:, C_SELQ:C_SELQ + 8 * P], ACT.Copy).then_inc(S["const_ready"], 1)
            act.activation(sel_k[:].rearrange("p a b -> p (a b)"), const[:, C_SELK:C_SELK + 8 * P], ACT.Copy).then_inc(S["const_ready"], 1)
            act.activation(w_hi[:], w_raw[:], ACT.Copy).then_inc(S["const_ready"], 1)
            act.wait_ge(S["mv_ready"], 1)
            act.activation(rstd[:], mv[:, :, 1], ACT.Sqrt, bias=keep["eps"][:]).then_inc(S["std_ready"], 1)
            act.activation(mw[:, 1:2], mw[:, 0:1], ACT.Exp, scale=-1.0).then_inc(S["std_ready"], 1)

            def step(g, other, kind, n):
                wait = waiter(act, g)
                if kind == "turn":
                    wait("xn_turned", n + 1)
                    wait("v_proj", 0)
                    wait("xn_saved", 0)
                    inc(act.activation(xn_hi[:, :, 2 * P * n:2 * P * n + 2 * P], PREP[:].rearrange("p (k n) -> p k n", k=KC), ACT.Copy), "xn_hi_done")
                elif kind == "q":
                    wait("q_done", n + 1)
                    wait("selected", 0)
                    inc(act.activation(q_hi[:, n, :], PREP[:], ACT.Copy), "q_hi_done")
                    wait("q_rec_step", 0)
                    inc(act.activation(q_neg[:, n, :], PREP[:], ACT.Tanh, scale=0.5), "q_tanh_done")
                    wait("q_tanh_done", n + 1)
                    inc(act.activation(q_neg[:, n, :], q_neg[:, n, :], ACT.Relu, scale=-2.0), "q_neg_done")
                elif kind == "k":
                    wait("k_done", 1)
                    wait("selected", 0)
                    inc(act.activation(k_b[:], PREP[:], ACT.Identity, scale=beta), "k_b_done")
                elif kind == "v":
                    wait("v_proj", 1)
                    if other is not None:
                        waiter(act, other)("pv_done", PAIRS)
                    inc(act.activation(V[:].rearrange("p t h c -> p (t h) c")[:, :, 0:DH], prep_bank(other, kind, n)[:, 0:TPG * DKV].rearrange("p (h d) -> p h d", d=DH), ACT.Copy), "v_done")
                elif (kind, n) in SEL_ACT:
                    select(act, g, other, kind, n)

            def unit(g, slot, between):
                wait = waiter(act, g)
                if slot >= 4 and slot % 2 == 0:
                    pr = slot // 2 - 2
                    wait("pv_done", pr + 1)
                    wait("o_turned", pr - 1)
                    inc(act.activation(o_sb[:, pr % 2, :], banks[4][:], ACT.Copy), "pv_copied")
                for j in range(4):
                    if 0 <= slot < UNITS:
                        wait("st_done", 4 * slot + j + 1)
                        if j == 0:
                            wait("pv_done", (slot - 4) // 2 + 1)
                        inc(act.activation(probs[:, slot % 4, j // 2, j % 2, :], banks[2 + j % 2][:], ACT.Exp, scale=SCALE), "probs_done")
                    if j % 2:
                        between(j // 2)

            run_turns(act, unit, step)

        @block.vector
        def _(dve):
            for t in range(TILES):
                if t % TPG == 0:
                    dve.wait_ge(S[f"xloaded{t // TPG}"], 16)
                dve.bn_stats(stats[:, t, :], X[:, t, :]).then_inc(S["stats_done"], 1)
            for t in range(TILES):
                dve.wait_ge(S["stats_done"], t + 1)
                last = dve.bn_aggr(mv[:, t, :], stats[:, t, :])
            last.then_inc(S["mv_ready"], 1)
            dve.wait_ge(S["const_ready"], 4)
            dve.tensor_tensor(w_lo[:], w_raw[:], w_hi[:].bitcast(F32), ALU.subtract).then_inc(S["w_ready"], 1)
            dve.wait_ge(S["std_ready"], 1)
            dve.reciprocal(rstd[:], rstd[:]).then_inc(S["rstd_ready"], 1)
            dve.wait_ge(S["std_ready"], 2)
            dve.tensor_scalar(mw[:, 2:3], mw[:, 1:2], 1.0, None, ALU.add).then_inc(S["mw_ready"], 1)
            dve.wait_ge(S["mw_ready"], 1)
            dve.reciprocal(mw[:, 2:3], mw[:, 2:3]).then_inc(S["mw_ready"], 1)
            dve.wait_ge(S["mw_ready"], 2)
            dve.tensor_scalar(mw[:, 3:4], mw[:, 2:3], -1.0, 1.0, ALU.mult, ALU.add).then_inc(S["mw_ready"], 1)
            dve.wait_ge(S["mw_ready"], 3)
            dve.wait_ge(S["rstd_ready"], 1)
            dve.wait_ge(S["const_ready"], 3)

            def step(g, other, kind, n):
                wait = waiter(dve, g)
                if kind == "normalise":
                    wait("xn_turned", n)
                    for t in range(2 * n, 2 * n + 2):
                        one = tile(g, t)
                        inc(dve.tensor_scalar(xn[:, t % 2, :, :], X[:, one, :].rearrange("p a (j k) -> p (a k) j", k=KC),
                                              mv[:, one, 0], rstd[:, one], ALU.subtract, ALU.mult), "xn_ready")
                elif kind == "turn":
                    wait("xn_hi_done", n + 1)
                    at = slice(2 * P * n, 2 * P * n + 2 * P)
                    inc(dve.tensor_tensor(xn_lo[:, :, at], PREP[:].rearrange("p (k n) -> p k n", k=KC), xn_hi[:, :, at].bitcast(F32), ALU.subtract), "xn_lo_done")
                elif kind == "q":
                    wait("q_tanh_done", n + 1)
                    inc(dve.tensor_tensor(q_lo[:, n, :], PREP[:], q_hi[:, n, :].bitcast(F32), ALU.subtract), "q_lo_done")
                    wait("mem_mm", 0)
                    inc(dve.tensor_scalar(sigma[:, n, :], PREP[:], 0.0, None, ALU.max), "q_relu_done")
                elif kind == "reciprocal":
                    wait("q_neg_done", n + 1)
                    inc(dve.tensor_scalar(q_rec[:, n, :], q_neg[:, n, :], 0.5, 1.0, ALU.mult, ALU.add), "q_rec_step")
                    wait("q_rec_step", n + 1)
                    inc(dve.reciprocal(q_rec[:, n, :], q_rec[:, n, :]), "q_rec_done")
                elif kind == "k":
                    wait("k_b_done", 1)
                    inc(dve.scalar_tensor_tensor(out=k_parts[:], in0=PREP[:], scalar=alpha, in1=k_b[:].bitcast(F32),
                                                 op0=ALU.mult, op1=ALU.add), "k_parts_done")
                elif kind == "memory":
                    am = prep_bank(other, kind, n)[:, 0:2 * 2 * (DKV + 1)].rearrange("p (q n) -> p q n", n=DKV + 1)
                    wait("mem_mm", n + 1)
                    wait("mem_done", 3 * n)
                    inc(dve.reciprocal(a_rec[:], am[:, :, DKV]), "mem_done")
                    wait("mem_done", 3 * n + 1)
                    inc(dve.tensor_tensor(a_mem[:].rearrange("p (q n) -> p q n", n=DKV), am[:, :, 0:DKV],
                                          a_rec[:].rearrange("p (q n) -> p q n", n=1).to_broadcast([P, 4, DKV]), ALU.mult), "mem_done")
                    wait("mem_done", 3 * n + 2)
                    xt = X[:, tile(g, n), :].rearrange("p a d -> p (a d)")
                    inc(dve.scalar_tensor_tensor(out=xt, in0=a_mem[:], scalar=mw[:, 2:3], in1=xt, op0=ALU.mult, op1=ALU.add), "mem_done")
                elif (kind, n) in SEL_DVE:
                    select(dve, g, other, kind, n)

            def decode(g, n):
                wait = waiter(dve, g)
                c, part = codes[n], code_part[:]
                wait("codes_loaded", 32)
                wait("decoded", 5 * n)
                inc(dve.tensor_scalar(part, c, 4, 0xF00, ALU.logical_shift_left, ALU.bitwise_and), "decoded")
                wait("decoded", 5 * n + 1)
                inc(dve.scalar_tensor_tensor(out=c, in0=c, scalar=0xF, in1=part, op0=ALU.bitwise_and, op1=ALU.bitwise_or), "decoded")
                wait("decoded", 5 * n + 2)
                inc(dve.tensor_scalar(part, c, 0x808, 4, ALU.bitwise_and, ALU.logical_shift_left), "decoded")
                inc(dve.tensor_scalar(c, c, 0x707, 2, ALU.bitwise_and, ALU.logical_shift_left), "decoded")
                wait("decoded", 5 * n + 4)
                pair = g * 2 + n
                pair = slice(pair, pair + 1) if isinstance(g, int) else bass.ds(pair, 1)
                inc(dve.tensor_tensor(keep["code_bytes"][:, pair, :].rearrange("p a n -> p (a n)"), c, part, ALU.add), "decoded")

            def turned_max(g, u):
                wait = waiter(dve, g)
                wait("max_turned", u + 1)
                wait("max_placed", 32 * (u - 1))
                wait("st_done", 4 * (u - 1))
                inc(dve.tensor_copy(max_parts[:, u % 2, 0, :], banks[6][0:8, 0:P]), "max_hi_done")
                wait("max_hi_done", u + 1)
                inc(dve.tensor_tensor(max_parts[:, u % 2, 1, :], banks[6][0:8, 0:P], max_parts[:, u % 2, 0, :].bitcast(F32),
                                      ALU.subtract), "max_split")

            def unit(g, slot, between):
                wait = waiter(dve, g)
                u = slot + 2
                for j in range(4):
                    if u < UNITS:
                        wait("s_done", 4 * u + j + 1)
                        if j == 0:
                            wait("max_turned", u - 1)
                        inc(dve.tensor_reduce(neg_max[:, u % 2, 2 * j:2 * j + 2], banks[j % 2][:].rearrange("p (s n) -> p s n", s=2),
                                              AX_X, ALU.max, negate=True), "max_done")
                    if j == 1 and 1 <= u <= UNITS:
                        turned_max(g, u - 1)
                    if j % 2:
                        between(j // 2)
                if slot in DECODE_AT:
                    decode(g, DECODE_AT.index(slot))
                if slot >= 4 and slot % 2 == 0:
                    pr = slot // 2 - 2
                    ot = banks[7][:].rearrange("p (l s g c) -> p l s g c", l=2, s=2, g=4)
                    wait("o_turned", pr + 1)
                    wait("o_normed", 5 * pr)
                    inc(dve.reciprocal(o_rec[:], banks[7][:].rearrange("p (g c) -> p g c", c=32)[:, :, DH]), "o_normed")
                    wait("o_normed", 5 * pr + 1)
                    rec = o_rec[:].rearrange("p (l s g a) -> p l s g a", l=2, s=2, a=1)
                    for s in range(2):
                        for v in range(2):
                            h, b = divmod(2 * pr + v, BPG)
                            out = att[:, 2 * b + s, :].rearrange("p (g l h d) -> p l g h d", g=2, l=2, h=HEADS)[:, :, :, h, :]
                            inc(dve.tensor_tensor(out, ot[:, :, s, 2 * v:2 * v + 2, 0:DH],
                                                  rec[:, :, s, 2 * v:2 * v + 2, :].to_broadcast([P, 2, 2, DH]), ALU.mult), "o_normed")
                if slot == SLOTS - 1:
                    wait("o_normed", 5 * PAIRS)
                    xg = X[:, tile(g, 0, TPG), :]
                    inc(dve.scalar_tensor_tensor(out=xg, in0=att[:], scalar=mw[:, 3:4], in1=xg, op0=ALU.mult, op1=ALU.add), "x_updated")

            run_turns(dve, unit, step)
            dve.wait_ge(S["x_updated"], START + GROUPS)

        @block.tensor
        def _(pe):
            pe.wait_ge(S["const_ready"], 3)
            pe.wait_ge(S["w_ready"], 1)
            pe.wait_ge(S["zeroed"], 4)
            pe.wait_ge(S["loaded"], 16 * 7)

            def product(out, cols, moving):
                n = 0
                for w, x in ((w_hi, xn_hi), (w_lo, xn_hi), (w_hi, xn_lo)):
                    for k in range(KC):
                        wk, xk = w[:, k, cols], x[:, k, moving]
                        lhs, rhs = (wk, xk) if moving == slice(0, GT) else (xk, wk)
                        mm = pe.matmul(out, lhs, rhs, start=(n == 0), stop=(n == 3 * KC - 1))
                        n += 1
                return mm

            def step(g, other, kind, n):
                wait = waiter(pe, g)
                if kind == "turn":
                    wait("xn_ready", 2 * n + 2)
                    if n == 0:
                        wait("sel_act", 0)
                        wait("sel_dve", 0)
                    else:
                        wait("xn_lo_done", n)
                    for t in range(2):
                        for k in range(KC):
                            mm = pe.transpose(PREP[:, 2 * P * k + P * t:2 * P * k + P * t + P], xn[:, t, k, :], ident[:])
                    inc(mm, "xn_turned")
                elif kind == "q":
                    wait("xn_lo_done", 2)
                    wait("q_relu_done", n)
                    wait("q_tanh_done", n)
                    inc(product(PREP[:], slice(P * n, P * n + P), slice(0, GT)), "q_done")
                elif kind == "k":
                    wait("q_relu_done", 2)
                    wait("q_tanh_done", 2)
                    inc(product(PREP[:], slice(D, D + P), slice(0, GT)), "k_done")
                elif kind == "v":
                    previous_done(wait, other, kind, n)
                    bank = prep_bank(other, kind, n)
                    for t in range(TPG):
                        mm = product(bank[:, DKV * t:DKV * t + DKV], slice(D + P, QKV), slice(P * t, P * t + P))
                    inc(mm, "v_proj")
                elif kind == "memory":
                    previous_done(wait, other, kind, n)
                    bank = prep_bank(other, kind, n)
                    wait("sigma_done", 2)
                    for c in range(2):
                        mm = pe.matmul(bank[:, 2 * (DKV + 1) * c:2 * (DKV + 1) * (c + 1)],
                                       sigma[:, c, P * n:P * n + P], mem2[:].rearrange("p a b -> p (a b)"), start=True, stop=True)
                    inc(mm, "mem_mm")
                elif kind in ("selk", "selq"):
                    previous_done(wait, other, kind, n)
                    bank = prep_bank(other, kind, n)
                    if kind == "selk":
                        wait("k_parts_done", 1)
                        inc(pe.matmul(bank[:], sel_k[:, n, :], k_parts[:], start=True, stop=True), "selected")
                    else:
                        wait("q_lo_done", 2)
                        quad, q = divmod(n, QPK)
                        v = 2 * (2 * quad + q % 2)
                        pe.matmul(bank[:], sel_q[:, v, :], q_hi[:, q // 2, :], start=True, stop=False)
                        inc(pe.matmul(bank[:], sel_q[:, v + 1, :], q_lo[:, q // 2, :], start=False, stop=True), "selected")

            def previous_done(wait, other, kind, n):
                at = PREP_ORDER.index((kind, n))
                kind, n = PREP_ORDER[at - (3 if other is None else 1)]
                if kind == "k":
                    wait("k_parts_done", 1)
                elif kind == "memory":
                    wait("mem_done", 3 * n + 3)
                elif kind == "v":
                    wait("v_done", 1)
                    wait("mem_done", 3 * TPG)
                else:
                    selections_done(wait, [(kind, n)])

            def scores(g, u, j):
                wait = waiter(pe, g)
                h, b = divmod(u, BPG)
                if j == 0 and b == 0:
                    selections_done(wait, [("selk", h)] + [("selq", h // 4 * QPK + n) for n in range(QPK)])
                wait("max_done", 4 * u + j - 1)
                for s in range(2):
                    mm = pe.matmul(banks[j % 2][:, SEQ * s:SEQ * s + SEQ], Q[0:ROWS, h // 4, b, j, P * s:P * s + P],
                                   K[0:ROWS, h, SEQ * b:SEQ * b + SEQ], start=True, stop=True)
                inc(mm, "s_done")

            def turn_max(g, u):
                wait = waiter(pe, g)
                wait("max_done", 4 * u + 4)
                wait("max_split", u)
                inc(pe.transpose(banks[6][0:8, 0:P], neg_max[:, u % 2, :], ident[:]), "max_turned")

            def scores_turned(g, u, j):
                wait = waiter(pe, g)
                h, b = divmod(u, BPG)
                if j == 0:
                    wait("max_placed", 32 * (u + 1))
                wait("probs_done", 4 * u + j - 1)
                th, qp = divmod(j, 2)
                inc(pe.matmul(banks[2 + j % 2][:].rearrange("p (q n) -> p q n", q=2), K[0:ROWS + 8, h, SEQ * b + P * th:SEQ * b + P * th + P],
                              Q[0:ROWS + 8, h // 4, b, 2 * qp:2 * qp + 2, :], start=True, stop=True), "st_done")

            def weighted(g, pr, part):
                wait = waiter(pe, g)
                half, th = divmod(part, 2)
                if part == 0:
                    wait("probs_done", 8 * pr + 8)
                    wait("pv_copied", pr)
                    if pr == 0:
                        wait("v_done", 1)
                at = slice(SEQ * half, SEQ * half + SEQ)
                for q in range(4):
                    u = 2 * pr + q // 2
                    h, b = divmod(u, BPG)
                    mm = pe.matmul(banks[4][32 * q:32 * q + 32, at], V[:, 2 * b + th, h, :],
                                   probs[:, u % 4, th, q % 2, at], start=(th == 0), stop=(th == 1), skip_group_check=True)
                if part == 3:
                    inc(mm, "pv_done")

            def turn_out(g, pr):
                wait = waiter(pe, g)
                wait("pv_copied", pr + 1)
                wait("o_normed", 5 * pr)
                for c in range(4):
                    mm = pe.transpose(banks[7][:, P * c:P * c + P], o_sb[:, pr % 2, P * c:P * c + P], ident[:])
                inc(mm, "o_turned")

            def unit(g, slot, between):
                for j in range(4):
                    if slot + 2 < UNITS:
                        scores(g, slot + 2, j)
                    if j == 1 and 0 <= slot + 1 < UNITS:
                        turn_max(g, slot + 1)
                    if 0 <= slot < UNITS:
                        scores_turned(g, slot, j)
                    if j % 2:
                        between(j // 2)
                        if 2 <= slot < UNITS + 2:
                            weighted(g, slot // 2 - 1, 2 * (slot % 2) + j // 2)
                    if j == 1 and slot >= 4 and slot % 2 == 0:
                        turn_out(g, slot // 2 - 2)

            run_turns(pe, unit, step)

        assert counted == PER, {n: (counted[n], PER[n]) for n in PER if counted[n] != PER[n]}


NVFP_BLOCK = 32
MLP = 2048
PAIRS_N = MLP // (2 * P)
WORDS = 3 * D
CHUNKS = MLP // P


L1_HEADS, L1_DH, TAPS = 16, 16, 4
PAD = TAPS - 1
FFN, FFN_CHUNKS = 704, 6
UPC = KC * FFN_CHUNKS * P
assert UPC == FFN_CHUNKS * D
TERNARY_PARTS = [slice(UPC * n, UPC * n + UPC) for n in range(3)]
C2_E, C2_CENTER, C2_COL = 0, P, 2 * P
N_CONST2 = 2 * P + 2
W_QK, W_V, W_IO, W_G, W_COLS = 0, 2 * D, 3 * D, 5 * D, 6 * D
G16, G256 = 4 * L1_DH, 2 * D
N_LOADS = 6
PAIR_HEADS = 2 * L1_HEADS


def layer0_mlp(nc, dram, keep):
    X, ident, x_hi, x_lo = keep["X"], keep["ident"], keep["xall_hi"], keep["xall_lo"]
    with ExitStack() as ctx:
        def sb(name, shape, dt=F32):
            return ctx.enter_context(nc.sbuf_tensor(name, shape, dt))

        code_bytes = keep["code_bytes"]
        scales = sb("scales", [P, 2, WORDS])
        w = sb("w", [P, 2, 2, WORDS])
        w_hi = sb("w2_hi", [P, PAIRS_N, 2, WORDS], F32R)
        w_lo = sb("w2_lo", [P, PAIRS_N, 2, WORDS], F32R)
        gelu = sb("gelu", [P, 2, GT])
        hid = sb("hid", [P, 2, GT])
        hid_hi = sb("hid_hi", [P, 2, GT], F32R)
        hid_lo = sb("hid_lo", [P, 2, GT], F32R)
        y = sb("y", [P, KC, GT])
        v_sum = sb("v_sum", [P, KC, L1_HEADS])
        threshold = sb("threshold", [P, 3, 4])

        banks = [ctx.enter_context(nc.psum_tensor(f"mbank{n}", [P, 512], F32)) for n in range(8)]
        gate_b, up_b, down_b, turn_b = banks[0:2], banks[2:4], banks[4:6], banks[6:8]
        names = """scales_even scales_odd raw_even raw_odd raw_used ternary_step centering w_done w_hi_done w_lo_done gate_done up_done gelu_done hid_done
            hid_hi_done hid_lo_done down_step y_done y_turned x_updated stats_done""".split()
        S = {n: ctx.enter_context(nc.semaphore(f"m_{n}")) for n in names}
        scale_sem = [S["scales_even"], S["scales_odd"]]
        raw_sem = [S["raw_even"], S["raw_odd"]]
        block = ctx.enter_context(nc.Block())
        C = CHUNKS

        @block.sync
        def _(sp):
            for a in range(PAIRS_N):
                if a == 2:
                    prime(sp, [S[n] for n in IN_LOOPS_1])
                if a >= 2:
                    sp.wait_ge(S["w_done"], a - 1)
                sp.dma_start(scales[:, a % 2, :], dram["scales"][:, a, :]).then_inc(scale_sem[a % 2], 16)
            sp.dma_start(keep["shared"][:], dram["l1w"].rearrange("p k n -> p (k n)")).then_inc(keep["raw_loaded"], 16)
            sp.wait_ge(S["w_lo_done"], PAIRS_N)
            for n in range(6):
                if n >= 2:
                    sp.wait_ge(S["raw_used"], n - 1)
                sp.dma_start(w[:, n % 2, :, :].rearrange("p a n -> p (a n)"), dram["ternary"][:, TERNARY_PARTS[n % 3]]).then_inc(raw_sem[n % 2], 16)

        def decode(dve, a):
            s = scales[:, a % 2, :]
            dve.wait_ge(scale_sem[a % 2], 16 * (a // 2 + 1))
            if a >= 2:
                dve.wait_ge(S["w_lo_done"], a - 1)
            values = code_bytes[:, a, :].bitcast(F8).rearrange("p (n b) -> p b n", b=2)
            dve.scalar_tensor_tensor(out=w[:, a % 2, 0, :], in0=values[:, 0, :], scalar=64.0, in1=s, op0=ALU.mult, op1=ALU.mult)
            dve.scalar_tensor_tensor(out=w[:, a % 2, 1, :], in0=values[:, 1, :], scalar=64.0, in1=s,
                                     op0=ALU.mult, op1=ALU.mult).then_inc(S["w_done"], 1)

        @block.gpsimd
        def _(pool):
            for a in range(PAIRS_N):
                pool.wait_ge(S["w_hi_done"], a + 1)
                pool.tensor_tensor(w_lo[:, a, :, :], w[:, a % 2, :, :], w_hi[:, a, :, :].bitcast(F32), ALU.subtract).then_inc(S["w_lo_done"], 1)
            w_raw = keep["shared"][:].rearrange("p (k n) -> p k n", k=KC)
            wv = w_raw[:, :, W_V:W_V + D].rearrange("p k (h d) -> p k h d", d=L1_DH)
            pool.wait_ge(keep["raw_loaded"], 16)
            steps = 0
            for d in range(1, L1_DH):
                if d > 1:
                    pool.wait_ge(S["centering"], steps)
                pool.tensor_tensor(v_sum[:], wv[:, :, :, 0] if d == 1 else v_sum[:], wv[:, :, :, d], ALU.add).then_inc(S["centering"], 1)
                steps += 1
            pool.wait_ge(S["centering"], steps)
            pool.tensor_scalar(v_sum[:], v_sum[:], -1.0 / L1_DH, None, ALU.mult).then_inc(S["centering"], 1)
            pool.wait_ge(S["centering"], steps + 1)
            for k in range(KC):
                mean = v_sum[:, k, :].rearrange("p (h a) -> p h a", a=1).to_broadcast([P, L1_HEADS, L1_DH])
                pool.tensor_tensor(wv[:, k], wv[:, k], mean, ALU.add).then_inc(S["centering"], 1)

            work = scales[:].rearrange("p a n -> p (a n)")
            thr = threshold
            done = [0]

            def step(ins):
                ins.then_inc(S["ternary_step"], 1)
                done[0] += 1
                pool.wait_ge(S["ternary_step"], done[0])

            def raw(n):
                pool.wait_ge(raw_sem[n % 2], 16 * (n // 2 + 1))
                return w[:, n % 2, :, :].rearrange("p a n -> p (a n)")

            for n in range(3):
                x = raw(n)
                step(pool.tensor_scalar(work, x, 0.0, 2.0, ALU.max, ALU.mult))
                step(pool.tensor_tensor(work, work, x, ALU.subtract))
                pool.sem_inc(S["raw_used"], 1)
                size = UPC
                while size % 2 == 0:
                    size //= 2
                    step(pool.tensor_tensor(work[:, 0:size], work[:, 0:size], work[:, size:2 * size], ALU.add))
                assert size == 3
                step(pool.tensor_tensor(work[:, 0:1], work[:, 0:1], work[:, 1:2], ALU.add))
                step(pool.tensor_tensor(thr[:, n, 3:4], work[:, 0:1], work[:, 2:3], ALU.add))
                step(pool.partition_all_reduce(thr[:, n, 0:1], thr[:, n, 3:4], P, bass.bass_isa.ReduceOp.add))
                step(pool.tensor_scalar(thr[:, n, 0:1], thr[:, n, 0:1], 1.0 / (FFN * D), 1e-8, ALU.mult, ALU.add))
                step(pool.tensor_scalar(thr[:, n, 1:2], thr[:, n, 0:1], 0.5, None, ALU.mult))
                step(pool.tensor_scalar(thr[:, n, 2:3], thr[:, n, 0:1], -0.5, None, ALU.mult))
            for n in range(3):
                x = raw(n + 3)
                step(pool.tensor_scalar(work, x, thr[:, n, 2:3], None, ALU.is_lt))
                step(pool.tensor_scalar(x, x, thr[:, n, 1:2], None, ALU.is_gt))
                step(pool.tensor_tensor(keep["rows"][:].bitcast(BF16)[:, TERNARY_PARTS[n]], x, work, ALU.subtract))
                pool.sem_inc(S["raw_used"], 1)

        @block.vector
        def _(dve):
            def turn(i, first):
                def hidden(c):
                    dve.wait_ge(S["gelu_done"], START + i * C + c + 1)
                    dve.wait_ge(S["up_done"], START + i * C + c + 1)
                    dve.wait_ge(S["hid_lo_done"], START + i * C + c - 1)
                    dve.tensor_tensor(hid[:, c % 2, :], gelu[:, c % 2, :], up_b[c % 2][:], ALU.mult).then_inc(S["hid_done"], 1)

                def hidden_lo(c):
                    dve.wait_ge(S["hid_hi_done"], START + i * C + c + 1)
                    dve.tensor_tensor(hid_lo[:, c % 2, :], hid[:, c % 2, :], hid_hi[:, c % 2, :].bitcast(F32),
                                      ALU.subtract).then_inc(S["hid_lo_done"], 1)

                for c in range(C):
                    if c >= 1:
                        hidden_lo(c - 1)
                    hidden(c)
                    if first and c % 2 == 0 and c // 2 + 2 < PAIRS_N:
                        decode(dve, c // 2 + 2)
                    if c == 1 and not first:
                        residual(i - 1)
                hidden_lo(C - 1)

            def residual(i):
                for t in range(TPG + 1):
                    if t < TPG:
                        dve.wait_ge(S["y_turned"], START + i * TPG + t + 1)
                        xt = X[:, bass.ds(i * TPG + t, 1), :].rearrange("p a d -> p (a d)")
                        dve.tensor_tensor(xt, turn_b[t % 2][:, 0:D], xt, ALU.add).then_inc(S["x_updated"], 1)
                    if t >= 1:
                        dve.wait_ge(S["x_updated"], START + i * TPG + t)
                        at = bass.ds(i * TPG + t - 1, 1)
                        dve.bn_stats(keep["stats"][:, at, :].rearrange("p a n -> p (a n)"),
                                     X[:, at, :].rearrange("p a d -> p (a d)")).then_inc(S["stats_done"], 1)

            decode(dve, 0)
            decode(dve, 1)
            turn(0, True)
            with dve.Fori(1, GROUPS) as i:
                turn(i, False)
            residual(GROUPS - 1)

        @block.scalar
        def _(act):
            def turn(i, first):
                def hidden_hi(c):
                    act.wait_ge(S["hid_done"], START + i * C + c + 1)
                    act.wait_ge(S["down_step"], START + i * C + c - 1)
                    act.activation(hid_hi[:, c % 2, :], hid[:, c % 2, :], ACT.Copy).then_inc(S["hid_hi_done"], 1)

                for c in range(C):
                    if c >= 1:
                        hidden_hi(c - 1)
                    act.wait_ge(S["gate_done"], START + i * C + c + 1)
                    act.wait_ge(S["hid_done"], START + i * C + c - 1)
                    act.activation(gelu[:, c % 2, :], gate_b[c % 2][:], ACT.Gelu_apprx_tanh).then_inc(S["gelu_done"], 1)
                    if first and c % 2 == 1 and c // 2 + 2 < PAIRS_N:
                        weights_hi(c // 2 + 2)
                    if c == 0 and not first:
                        result(i - 1)
                hidden_hi(C - 1)

            def result(i):
                act.wait_ge(S["y_turned"], START + i * TPG)
                for k in range(KC):
                    act.wait_ge(S["down_step"], START + i * C + C)
                    act.activation(y[:, k, :], down_b[k][:], ACT.Copy).then_inc(S["y_done"], 1)

            def weights_hi(a):
                act.wait_ge(S["w_done"], a + 1)
                act.activation(w_hi[:, a, :, :], w[:, a % 2, :, :], ACT.Copy).then_inc(S["w_hi_done"], 1)

            weights_hi(0)
            weights_hi(1)
            turn(0, True)
            with act.Fori(1, GROUPS) as i:
                turn(i, False)
            result(GROUPS - 1)

        @block.tensor
        def _(pe):
            def up(i, c, which, bank, done):
                a, m = divmod(c, 2)
                cols = slice(D * which + P * m, D * which + P * m + P)
                n = 0
                for wt, x in ((w_hi, x_hi), (w_lo, x_hi), (w_hi, x_lo)):
                    for k in range(KC):
                        mm = pe.matmul(bank[:], wt[:, a, k, cols], x[:, k, bass.ds(i * GT, GT)], start=(n == 0), stop=(n == 5))
                        n += 1
                mm.then_inc(done, 1)

            def down(i, c):
                a, m = divmod(c, 2)
                pe.wait_ge(S["hid_lo_done"], START + i * C + c + 1)
                if c == 0:
                    pe.wait_ge(S["y_done"], START + i * KC)
                for k in range(KC):
                    cols = slice(2 * D + P * k, 2 * D + P * k + P)
                    for n, (wt, h) in enumerate(((w_hi, hid_hi), (w_lo, hid_hi), (w_hi, hid_lo))):
                        mm = pe.matmul(down_b[k][:], wt[:, a, m, cols], h[:, c % 2, :],
                                       start=(c == 0 and n == 0), stop=(c == C - 1 and n == 2))
                mm.then_inc(S["down_step"], 1)

            def turn_y(i):
                for t in range(TPG):
                    if t == 0:
                        pe.wait_ge(S["y_done"], START + i * KC + KC)
                    pe.wait_ge(S["x_updated"], START + i * TPG + t - 1)
                    for k in range(KC):
                        mm = pe.transpose(turn_b[t % 2][:, P * k:P * k + P], y[:, k, P * t:P * t + P], ident[:])
                    mm.then_inc(S["y_turned"], 1)

            def turn(i, first):
                for c in range(C):
                    if first:
                        pe.wait_ge(S["w_lo_done"], c // 2 + 1)
                    pe.wait_ge(S["gelu_done"], START + i * C + c - 1)
                    up(i, c, 0, gate_b[c % 2], S["gate_done"])
                    pe.wait_ge(S["hid_done"], START + i * C + c - 1)
                    up(i, c, 1, up_b[c % 2], S["up_done"])
                    if c == 1 and not first:
                        turn_y(i - 1)
                    if c >= 1:
                        down(i, c - 1)
                    elif not first:
                        down(i - 1, C - 1)

            turn(0, True)
            with pe.Fori(1, GROUPS) as i:
                turn(i, False)
            down(GROUPS - 1, C - 1)
            turn_y(GROUPS - 1)


def layer1(nc, dram, keep, out):
    X, ident = keep["X"], keep["ident"]
    with ExitStack() as ctx:
        def sb(name, shape, dt=F32):
            return ctx.enter_context(nc.sbuf_tensor(name, shape, dt))

        const2 = sb("const2", [P, N_CONST2])
        ones_rows = sb("ones_rows", [P, P], F32R)
        center = const2[:, C2_CENTER:C2_CENTER + P]
        w_hi = sb("l1_hi", [P, KC, W_COLS], F32R)
        w_lo = sb("l1_lo", [P, KC, W_COLS], F32R)
        wo_hi = sb("wo_hi", [P, KC, D], F32R)
        wo_lo = sb("wo_lo", [P, KC, D], F32R)
        bias = sb("bias", [P, 2 * D], F32R)
        conv = sb("conv", [P, KC, TAPS + 1])
        gamma_b = sb("gamma_b", [P, KC])
        par = sb("par", [P, G16 + G256])
        vn_g, vn_b, mn_g, mn_b = (par[:, L1_DH * n:L1_DH * n + L1_DH].rearrange("p (a d) -> p a d", a=1)
                                  .to_broadcast([P, PAIR_HEADS, L1_DH]) for n in range(4))
        gn_g, gn_b = par[:, G16:G16 + D], par[:, G16 + D:G16 + 2 * D]
        gn_g2, gn_b2 = (x.rearrange("p (a d) -> p a d", a=1).to_broadcast([P, BPG, D]) for x in (gn_g, gn_b))
        tern = sb("tern", [P, 3 * UPC], F32R)
        parts = TERNARY_PARTS
        w1 = tern[:, parts[0]].rearrange("p (k n) -> p k n", k=KC)
        w2 = tern[:, parts[1]].rearrange("p (k n) -> p k n", k=KC)
        w3 = tern[:, parts[2]].rearrange("p (c n) -> p c n", n=D)
        half = sb("half", [P, TILES])
        eps16 = sb("eps16", [P, 3 * PAIR_HEADS])
        stats = keep["stats"]
        mv = sb("l1_mv", [P, TILES, 2])
        rstd = sb("l1_rstd", [P, TILES])
        PER = dict(xn_ready=TPG, xn_turned=BPG, xn_hi_done=BPG, xpad_done=BPG, xn_lo_done0=1, xn_lo_done1=1,
                   conv_step=8, conv_sig=KC, xc_done=KC, xc_hi_done=KC, xc_lo_done=KC,
                   qk_done=TPG, v_done=BPG, qk_copied=TPG, qk_sq=TPG, v_sq=BPG, ss_summed=BPG, norm_done=1, q_kept=1,
                   vn_done=BPG, gamma_done=KC, decay_done=KC, io_done=TPG, gates_done=TPG,
                   kv_link0=3, kv_link1=3, kv_done0=1, kv_done1=1, b_done0=1, b_done1=1,
                   up_done=FFN_CHUNKS, sig_done=FFN_CHUNKS, hid_done=FFN_CHUNKS, h_hi_done=FFN_CHUNKS,
                   **{f"h_lo_done{c}": 1 for c in range(FFN_CHUNKS)}, down_done=BPG, mlp_done=BPG,
                   b_turned=BPG, scan_done=BPG, mem_centered=BPG, mem_sq=BPG, sm_done=BPG, rm_done=1, mn_done=BPG,
                   op_link0=2, op_link1=2, op_done0=1, op_done1=1, so_done=BPG, cen_done=BPG, cen_sq=BPG, s2_done=BPG,
                   ro_done=1, on_done=BPG, o_link0=2, o_link1=2, o_done0=1, o_done1=1,
                   o_turned=BPG, o_hi_done=BPG, o_lo_done=BPG, y_done=BPG, res_done=BPG,
                   stored0=16, stored1=16, roots=10, roots_late=23)
        S = {n: ctx.enter_context(nc.semaphore(f"l_{n}")) for n in PER}
        with ExitStack() as prep:
            def tmp(name, shape, dt=F32):
                return prep.enter_context(nc.sbuf_tensor(name, shape, dt))

            w_raw = keep["shared"][:].rearrange("p (k n) -> p k n", k=KC)
            wo_raw = tmp("wo_raw", [P, KC, D])
            bias_raw = tmp("bias_raw", [P, 2 * D])
            bias_b = tmp("bias_b", [P, 2 * D], F32R)
            once = {n: prep.enter_context(nc.semaphore(f"l1_{n}")) for n in
                    "loaded zeroed w_hi_done w_lo_done bias_b_done ternary mv_done var_done rstd_done".split()}
            block = prep.enter_context(nc.Block())

            @block.sync
            def _(sp):
                sp.wait_ge(once["zeroed"], 1)
                loads = [(const2[:], dram["const2"]), (wo_raw[:], dram["wo"]),
                         (conv[:], dram["conv"]), (gamma_b[:], dram["gamma_b"])]
                loads.append((par[:], dram["scales_shifts"].partition_broadcast(P)))
                loads.append((bias_raw[0:2, :], dram["gate_bias"]))
                assert len(loads) == N_LOADS
                for dst, src in loads:
                    sp.dma_start(dst, src).then_inc(once["loaded"], 16)
                prime(sp, list(S.values()))

            @block.gpsimd
            def _(pool):
                pool.memset(bias_raw[:], 0.0).then_inc(once["zeroed"], 1)
                pool.memset(half[:], -0.5).then_inc(once["zeroed"], 1)
                pool.memset(eps16[:, 0:2 * PAIR_HEADS], 0.0).then_inc(once["zeroed"], 1)
                pool.memset(eps16[:, 2 * PAIR_HEADS:3 * PAIR_HEADS], L1_DH * EPS).then_inc(once["zeroed"], 1)
                pool.wait_ge(once["zeroed"], 4)
                pool.wait_ge(once["mv_done"], 1)
                pool.tensor_scalar(rstd[:], mv[:, :, 1], 1.0, EPS, ALU.mult, ALU.add).then_inc(once["var_done"], 1)
                pool.wait_ge(once["var_done"], 1)
                pool.tensor_tensor(rstd[:], rstd[:], half[:, 0:TILES], ALU.pow).then_inc(once["rstd_done"], 1)
                pool.wait_ge(once["loaded"], 16 * N_LOADS)
                for n in (0, 2):
                    scale = par[:, L1_DH * n:L1_DH * n + L1_DH]
                    pool.tensor_scalar(scale, scale, 4.0, None, ALU.mult)
                pool.tensor_scalar(gn_g, gn_g, 4.0, None, ALU.mult)
                pool.wait_ge(once["w_hi_done"], 2)
                pool.tensor_tensor(wo_lo[:], wo_raw[:], wo_hi[:].bitcast(F32), ALU.subtract).then_inc(once["w_lo_done"], 1)

            @block.scalar
            def _(act):
                act.activation(w_hi[:], w_raw[:], ACT.Copy).then_inc(once["w_hi_done"], 1)
                act.activation(tern[:], keep["rows"][:].bitcast(BF16)[:, 0:3 * UPC], ACT.Copy).then_inc(once["ternary"], 1)
                act.wait_ge(once["loaded"], 16 * N_LOADS)
                act.activation(ones_rows[:], const2[:, C2_E:C2_E + P], ACT.Copy).then_inc(once["bias_b_done"], 1)
                act.activation(bias_b[:], bias_raw[:], ACT.Identity, scale=const2[:, C2_COL + 1:C2_COL + 2]).then_inc(once["bias_b_done"], 1)
                act.activation(wo_hi[:], wo_raw[:], ACT.Copy).then_inc(once["w_hi_done"], 1)

            @block.vector
            def _(dve):
                for t in range(TILES):
                    ins = dve.bn_aggr(mv[:, t, :], stats[:, t, :])
                ins.then_inc(once["mv_done"], 1)
                dve.wait_ge(once["w_hi_done"], 1)
                dve.tensor_tensor(w_lo[:], w_raw[:], w_hi[:].bitcast(F32), ALU.subtract).then_inc(once["w_lo_done"], 1)
                dve.wait_ge(once["bias_b_done"], 2)
                dve.scalar_tensor_tensor(out=bias[:], in0=bias_raw[:], scalar=const2[:, C2_COL:C2_COL + 1], in1=bias_b[:].bitcast(F32),
                                         op0=ALU.mult, op1=ALU.add)

        xn = sb("l1_xn", [P, TPG, KC, P])
        xn_hi = sb("l1_xn_hi", [P, KC, GT], F32R)
        xn_lo = sb("l1_xn_lo", [P, KC, GT], F32R)
        xpad = sb("xpad", [P, KC, BPG, PAD + SEQ])
        cv, cs, decay = (keep["shared"][:, KC * GT * n:KC * GT * n + KC * GT].rearrange("p (k n) -> p k n", k=KC) for n in range(3))
        xc_hi = sb("xc_hi", [P, KC, GT], F32R)
        xc_lo = sb("xc_lo", [P, KC, GT], F32R)
        qk = sb("qk", [P, 2, TPG, D])
        sq = sb("sq", [P, BPG, 3, 2, D])
        ss = sb("ss", [P, BPG, 3 * PAIR_HEADS])
        rq = sb("rq", [P, BPG, PAIR_HEADS])
        q_kept = sb("q_kept", [P, TPG, D])
        vn, mem_rows, o = (keep["rows"][:, TPG * D * n:TPG * D * n + TPG * D] for n in range(3))
        vn, o = (x.rearrange("p (a d) -> p a d", d=D) for x in (vn, o))
        gates = sb("gates", [P, 2, TPG, D])
        mem = mem_rows.rearrange("p (k n) -> p k n", k=KC)
        sm = sb("sm", [P, BPG, PAIR_HEADS])
        so = sb("so", [P, BPG, PAIR_HEADS])
        s2 = sb("s2", [P, BPG, PAIR_HEADS])
        ry = sb("ry", [P, BPG * 3 * PAIR_HEADS])
        rt = sb("rt", [P, BPG * 3 * PAIR_HEADS])
        osq = sb("osq", [P, BPG, 2 * D])
        o_hi = sb("o_hi", [P, BPG, KC, SEQ], F32R)
        o_lo = sb("o_lo", [P, BPG, KC, SEQ], F32R)
        sig = sb("sig", [P, 2, GT])
        hid = sb("l1_hid", [P, 2, GT])
        h_hi = sb("h_hi", [P, FFN_CHUNKS, GT], F32R)
        h_lo = sb("h_lo", [P, FFN_CHUNKS, GT], F32R)
        res = sb("res", [P, BPG, 2, D])

        banks = [ctx.enter_context(nc.psum_tensor(f"lbank{n}", [P, 512], F32)) for n in range(8)]
        pad_zeroed = ctx.enter_context(nc.semaphore("pad_zeroed"))
        block = ctx.enter_context(nc.Block())
        counted = dict.fromkeys(PER, 0)

        def inc(ins, name, by=1):
            counted[name] += by
            ins.then_inc(S[name], by)

        def pair(b):
            return slice(2 * b, 2 * b + 2)

        def flat(ap):
            return ap.rearrange("p a d -> p (a d)")

        def heads(ap):
            return ap.rearrange("p a (h d) -> p (a h) d", d=L1_DH)

        def turned(ap):
            return ap.rearrange("p (k n) -> p k n", k=KC)

        def each(ap):
            return ap.rearrange("p (h a) -> p h a", a=1).to_broadcast([P, PAIR_HEADS, L1_DH])

        def waiter(engine, g):
            def wait(name, k):
                engine.wait_ge(S[name], START + g * PER[name] + k)
            return wait

        def turns(engine, turn):
            before = dict(counted)
            turn(None, 0)
            counted.update(before)
            with engine.Fori(0, GROUPS - 1) as i:
                turn(i, i + 1)
            whole = dict(counted)
            turn(GROUPS - 1, None)
            counted.update(whole)


        def linked(engine, wait, name, steps):
            for n, step in enumerate(steps):
                if n:
                    wait(name, n)
                ins = engine.tensor_tensor(*step)
                if n + 1 < len(steps):
                    inc(ins, name)
            return ins

        def xn_low(engine, early, b):
            wait = waiter(engine, early)
            wait("xpad_done", b + 1)
            wait("v_done", 0)
            wait("up_done", 0)
            at = slice(SEQ * b, SEQ * b + SEQ)
            inc(engine.tensor_tensor(xn_lo[:, :, at], xpad[:, :, b, PAD:PAD + SEQ], xn_hi[:, :, at].bitcast(F32), ALU.subtract), f"xn_lo_done{b}")

        def hidden_low(engine, early, c):
            wait = waiter(engine, early)
            wait("h_hi_done", c + 1)
            inc(engine.tensor_tensor(h_lo[:, c, :], hid[:, c % 2, :], h_hi[:, c, :].bitcast(F32), ALU.subtract), f"h_lo_done{c}")

        def values(engine, early, b):
            wait = waiter(engine, early)
            wait("vn_done", b + 1)
            wait("qk_copied", 2 * b + 2)
            v, k = vn[:, pair(b), :], qk[:, 1, pair(b), :]
            inc(linked(engine, wait, f"kv_link{b}", [
                (heads(v), heads(v), vn_g, ALU.mult),
                (heads(v), heads(v), vn_b, ALU.add),
                (heads(k), heads(k), each(ss[:, b, PAIR_HEADS:2 * PAIR_HEADS]), ALU.mult),
                (k, k, v, ALU.mult)]), f"kv_done{b}")

        def through_input_gate(engine, early, b):
            wait = waiter(engine, early)
            wait("gates_done", 2 * b + 2)
            wait(f"kv_done{b}", 1)
            inc(engine.tensor_tensor(vn[:, pair(b), :], qk[:, 1, pair(b), :], gates[:, 0, pair(b), :], ALU.mult), f"b_done{b}")

        def memory_scaled(engine, late, b):
            wait = waiter(engine, late)
            wait("mn_done", b + 1)
            wait("q_kept", 1)
            y = o[:, pair(b), :]
            inc(linked(engine, wait, f"op_link{b}", [
                (heads(y), heads(y), mn_g, ALU.mult),
                (heads(y), heads(y), mn_b, ALU.add),
                (y, y, q_kept[:, pair(b), :], ALU.mult)]), f"op_done{b}")

        def gated(engine, late, b):
            wait = waiter(engine, late)
            wait("on_done", b + 1)
            y = o[:, pair(b), :]
            inc(linked(engine, wait, f"o_link{b}", [
                (y, y, gn_g2, ALU.mult),
                (y, y, gn_b2, ALU.add),
                (y, y, gates[:, 1, pair(b), :], ALU.mult)]), f"o_done{b}")

        @block.sync
        def _(sp):
            with sp.Fori(0, GROUPS) as i:
                at = sp.snap(i * GT)
                for b in range(BPG):
                    sp.wait_ge(S["res_done"], START + i * PER["res_done"] + b + 1)
                    inc(sp.dma_start(out[bass.ds(at + SEQ * b, SEQ), :].rearrange("(a p) d -> p a d", p=P), res[:, b, :, :]), f"stored{b}", 16)
            for n in range(2):
                sp.wait_ge(S[f"stored{n}"], START + 16 * GROUPS)

        @block.gpsimd
        def _(pool):
            pool.memset(xpad[:, :, :, 0:PAD], 0.0).then_inc(pad_zeroed, 1)

            def turn(late, early):
                def convolved():
                    wait = waiter(pool, early)
                    for k in range(KC):
                        wait("conv_sig", k + 1)
                        inc(pool.tensor_tensor(cs[:, k, :], cv[:, k, :], cs[:, k, :], ALU.mult), "xc_done")
                    for k in range(KC):
                        wait("xc_hi_done", k + 1)
                        inc(pool.tensor_tensor(xc_lo[:, k, :], cs[:, k, :], xc_hi[:, k, :].bitcast(F32), ALU.subtract), "xc_lo_done")

                if early is not None:
                    xn_low(pool, early, 1)
                if late is not None:
                    memory_scaled(pool, late, 1)
                if early is not None:
                    hidden_low(pool, early, 1)
                    convolved()
                    hidden_low(pool, early, 2)
                    values(pool, early, 0)
                    hidden_low(pool, early, 3)
                if late is not None:
                    gated(pool, late, 0)
                if early is not None:
                    hidden_low(pool, early, 4)
                    hidden_low(pool, early, 5)
                    through_input_gate(pool, early, 0)
                    through_input_gate(pool, early, 1)

            turns(pool, turn)

        @block.scalar
        def _(act):
            act.wait_ge(pad_zeroed, 1)

            def turn(late, early):
                def xn_high(b):
                    wait = waiter(act, early)
                    wait("xn_turned", b + 1)
                    if b == 0:
                        wait("v_done", 0)
                        wait("up_done", 0)
                        wait("conv_step", 0)
                        wait("xn_lo_done0", 0)
                        wait("xn_lo_done1", 0)
                    src = turned(banks[b][:])
                    inc(act.activation(xn_hi[:, :, SEQ * b:SEQ * b + SEQ], src, ACT.Copy), "xn_hi_done")
                    inc(act.activation(xpad[:, :, b, PAD:PAD + SEQ], src, ACT.Copy), "xpad_done")

                def projected(t):
                    wait = waiter(act, early)
                    wait("qk_done", t + 1)
                    if t == 0:
                        wait("ss_summed", 0)
                        wait("b_done0", 0)
                        wait("b_done1", 0)
                    inc(act.activation(qk[:, :, t, :], turned(banks[2 + t % 2][:]), ACT.Copy), "qk_copied")
                    inc(act.activation(sq[:, t // 2, 0:2, t % 2, :], turned(banks[2 + t % 2][:]), ACT.Square), "qk_sq")

                def values_squared(b):
                    wait = waiter(act, early)
                    wait("v_done", b + 1)
                    inc(act.activation(sq[:, b, 2, :, :], turned(banks[b][:]), ACT.Square), "v_sq")

                def hidden(c):
                    if c > 0:
                        hidden_high(c - 1)
                    sigmoid(c)

                def sigmoid(c):
                    wait = waiter(act, early)
                    wait("up_done", c + 1)
                    inc(act.activation(sig[:, c % 2, :], banks[6][:], ACT.Sigmoid), "sig_done")

                def hidden_high(c):
                    wait = waiter(act, early)
                    wait("hid_done", c + 1)
                    if c == 0:
                        wait("down_done", 0)
                    inc(act.activation(h_hi[:, c, :], hid[:, c % 2, :], ACT.Copy), "h_hi_done")

                def convolved():
                    wait = waiter(act, early)
                    for k in range(KC):
                        wait("conv_step", 7 + k)
                        inc(act.activation(cs[:, k, :], cv[:, k, :], ACT.Sigmoid), "conv_sig")
                    wait("io_done", 0)
                    for k in range(KC):
                        wait("xc_done", k + 1)
                        inc(act.activation(xc_hi[:, k, :], cs[:, k, :], ACT.Copy), "xc_hi_done")

                def decays(m):
                    wait = waiter(act, early)
                    wait("gamma_done", m + 1)
                    if m == 0:
                        wait("scan_done", 0)
                    inc(act.activation(decay[:, m, :], banks[m][:], ACT.Sigmoid, bias=gamma_b[:, m:m + 1]), "decay_done")

                def queries_kept():
                    wait = waiter(act, early)
                    wait("norm_done", 1)
                    wait("op_done0", 0)
                    wait("op_done1", 0)
                    wait("ro_done", 0)
                    act.activation(q_kept[:], qk[:, 0, :, :], ACT.Copy)
                    inc(act.activation(rq[:], ss[:, :, 0:PAIR_HEADS], ACT.Copy), "q_kept")

                def gate(t):
                    wait = waiter(act, early)
                    wait("io_done", t + 1)
                    if t == 0:
                        wait("o_done0", 0)
                        wait("o_done1", 0)
                        wait("b_done0", 0)
                        wait("b_done1", 0)
                    inc(act.activation(gates[:, :, t, :], turned(banks[2 + t % 2][:]), ACT.Sigmoid), "gates_done")

                def memory_squared(b):
                    wait = waiter(act, late)
                    wait("mem_centered", b + 1)
                    inc(act.activation(osq[:, b, :], banks[4 + b][:], ACT.Square), "mem_sq")

                def output_squared(b):
                    wait = waiter(act, late)
                    wait("cen_done", b + 1)
                    inc(act.activation(osq[:, b, :], flat(o[:, pair(b), :]), ACT.Square), "cen_sq")

                def output_high(b):
                    wait = waiter(act, late)
                    wait("o_turned", b + 1)
                    inc(act.activation(o_hi[:, b, :, :], turned(banks[4 + b][:]), ACT.Copy), "o_hi_done")

                if early is not None:
                    xn_high(0)
                    xn_high(1)
                if late is not None:
                    memory_squared(0)
                if early is not None:
                    projected(0)
                    projected(1)
                if late is not None:
                    memory_squared(1)
                if early is not None:
                    hidden(0)
                    hidden(1)
                    projected(2)
                    values_squared(0)
                    values_squared(1)
                    hidden(2)
                    projected(3)
                    hidden(3)
                    convolved()
                if late is not None:
                    output_squared(0)
                    output_squared(1)
                if early is not None:
                    decays(0)
                    hidden_high(3)
                    sigmoid(4)
                    queries_kept()
                    hidden(5)
                    gate(0)
                    gate(1)
                if late is not None:
                    output_high(0)
                if early is not None:
                    hidden_high(5)
                if late is not None:
                    output_high(1)
                if early is not None:
                    decays(1)
                    gate(2)
                    gate(3)

            turns(act, turn)

        @block.vector
        def _(dve):
            def turn(late, early):
                links = [0, 0]

                def link(ins, g, which):
                    links[which] += 1
                    inc(ins, ("roots", "roots_late")[which])
                    waiter(dve, g)(("roots", "roots_late")[which], links[which])

                def inverse_root(x, g, which, done):
                    n = x.shape[-1]
                    y, t = ry[:, 0:n], rt[:, 0:n]
                    link(dve.tensor_scalar(y.bitcast(I32), x.bitcast(I32), -0.5, float(0x5f3759df), ALU.mult, ALU.add), g, which)
                    for step in range(3):
                        link(dve.tensor_tensor(t, x, y, ALU.mult), g, which)
                        link(dve.scalar_tensor_tensor(out=t, in0=t, scalar=-0.5, in1=y, op0=ALU.mult, op1=ALU.mult), g, which)
                        ins = dve.scalar_tensor_tensor(out=x if step == 2 else y, in0=t, scalar=1.5, in1=y, op0=ALU.add, op1=ALU.mult)
                        if step == 2 and done:
                            inc(ins, done)
                        else:
                            link(ins, g, which)

                def normalise():
                    wait = waiter(dve, early)
                    wait("xn_turned", 0)
                    for t in range(TPG):
                        at = early * TPG + t
                        one = slice(at, at + 1) if isinstance(early, int) else bass.ds(at, 1)
                        x = flat(X[:, one, :]).rearrange("p (j k) -> p k j", k=KC)
                        inc(dve.tensor_scalar(xn[:, t, :, :], x, mv[:, one, 0], rstd[:, one], ALU.subtract, ALU.mult), "xn_ready")

                def convolve():
                    wait = waiter(dve, early)
                    wait("xpad_done", BPG)
                    wait("xc_lo_done", 0)
                    n = 0
                    for tap in range(TAPS):
                        for k in range(KC):
                            src = xpad[:, k, :, tap:tap + SEQ]
                            dst = cv[:, k, :].rearrange("p (b s) -> p b s", b=BPG)
                            if tap == 0:
                                ins = dve.tensor_scalar(dst, src, conv[:, k, 0:1], conv[:, k, TAPS:TAPS + 1], ALU.mult, ALU.add)
                            else:
                                wait("conv_step", n - 1)
                                ins = dve.scalar_tensor_tensor(out=dst, in0=src, scalar=conv[:, k, tap:tap + 1], in1=dst, op0=ALU.mult, op1=ALU.add)
                            inc(ins, "conv_step")
                            n += 1

                def norms():
                    wait = waiter(dve, early)
                    wait("kv_done0", 0)
                    wait("kv_done1", 0)
                    wait("q_kept", 0)
                    for b in range(BPG):
                        wait("qk_sq", 2 * b + 2)
                        wait("v_sq", b + 1)
                        inc(dve.tensor_reduce(ss[:, b, :], sq[:, b, :, :, :].rearrange("p c a (h d) -> p (c a h) d", d=L1_DH), AX_X, ALU.add), "ss_summed")
                    wait("ss_summed", BPG)
                    link(dve.scalar_tensor_tensor(out=ss[:], in0=ss[:], scalar=1e-24,
                                                  in1=eps16[:].rearrange("p (a n) -> p a n", a=1).to_broadcast([P, BPG, 3 * PAIR_HEADS]),
                                                  op0=ALU.max, op1=ALU.add), early, 0)
                    inverse_root(flat(ss[:]), early, 0, "norm_done")
                    wait("norm_done", 1)
                    wait("b_turned", 0)
                    for b in range(BPG):
                        inc(dve.tensor_tensor(heads(vn[:, pair(b), :]), heads(turned(banks[b][:])), each(ss[:, b, 2 * PAIR_HEADS:]), ALU.mult), "vn_done")

                def hidden(c):
                    wait = waiter(dve, early)
                    wait("sig_done", c + 1)
                    if c >= 2:
                        wait(f"h_lo_done{c - 2}", 1)
                    inc(dve.tensor_tensor(hid[:, c % 2, :], sig[:, c % 2, :], banks[7][:], ALU.mult), "hid_done")

                def mlp_added(b):
                    wait = waiter(dve, early)
                    wait("down_done", b + 1)
                    at = early * TPG + 2 * b
                    x = X[:, slice(at, at + 2) if isinstance(early, int) else bass.ds(at, 2), :]
                    inc(dve.tensor_tensor(x, x, turned(banks[6 + b][:]), ALU.add), "mlp_done")

                def scan(b):
                    wait = waiter(dve, late)
                    wait("b_turned", b + 1)
                    wait("decay_done", KC)
                    wait("mem_centered", 0)
                    for m in range(KC):
                        ins = dve.tensor_tensor_scan(mem[:, m, SEQ * b:SEQ * b + SEQ], decay[:, m, SEQ * b:SEQ * b + SEQ],
                                                     banks[4 + b][:, SEQ * m:SEQ * m + SEQ], 0.0, ALU.mult, ALU.add)
                    inc(ins, "scan_done")

                def memory_normed():
                    wait = waiter(dve, late)
                    for b in range(BPG):
                        wait("mem_sq", b + 1)
                        inc(dve.tensor_reduce(sm[:, b, :], osq[:, b, :].rearrange("p (h d) -> p h d", d=L1_DH), AX_X, ALU.add), "sm_done")
                    wait("sm_done", BPG)
                    link(dve.tensor_scalar(sm[:], sm[:], L1_DH * EPS, None, ALU.add), late, 1)
                    inverse_root(flat(sm[:]), late, 1, "rm_done")
                    wait("rm_done", 1)
                    wait("o_turned", 0)
                    for b in range(BPG):
                        inc(dve.tensor_tensor(heads(o[:, pair(b), :]), heads(turned(banks[4 + b][:])), each(sm[:, b, :]), ALU.mult), "mn_done")

                def output_centered(b):
                    wait = waiter(dve, late)
                    wait(f"op_done{b}", 1)
                    inc(dve.tensor_reduce(so[:, b, :], heads(o[:, pair(b), :]), AX_X, ALU.add), "so_done")
                    wait("so_done", b + 1)
                    inc(dve.scalar_tensor_tensor(out=heads(o[:, pair(b), :]), in0=each(so[:, b, :]), scalar=-1.0 / L1_DH, in1=heads(o[:, pair(b), :]),
                                                 op0=ALU.mult, op1=ALU.add), "cen_done")

                def output_normed():
                    wait = waiter(dve, late)
                    for b in range(BPG):
                        wait("cen_sq", b + 1)
                        inc(dve.tensor_reduce(s2[:, b, :], osq[:, b, :].rearrange("p (h d) -> p h d", d=L1_DH), AX_X, ALU.add), "s2_done")
                    wait("s2_done", BPG)
                    wait("q_kept", 1)
                    link(dve.tensor_tensor(s2[:], s2[:], rq[:], ALU.mult), late, 1)
                    link(dve.tensor_tensor(s2[:], s2[:], rq[:], ALU.mult), late, 1)
                    link(dve.tensor_scalar(s2[:], s2[:], L1_DH * EPS, None, ALU.add), late, 1)
                    inverse_root(flat(s2[:]), late, 1, None)
                    inc(dve.tensor_tensor(s2[:], s2[:], rq[:], ALU.mult), "ro_done")
                    wait("ro_done", 1)
                    for b in range(BPG):
                        inc(dve.tensor_tensor(heads(o[:, pair(b), :]), heads(o[:, pair(b), :]), each(s2[:, b, :]), ALU.mult), "on_done")

                def output_low(b):
                    wait = waiter(dve, late)
                    wait("o_hi_done", b + 1)
                    inc(dve.tensor_tensor(o_lo[:, b, :, :], turned(banks[4 + b][:]), o_hi[:, b, :, :].bitcast(F32), ALU.subtract), "o_lo_done")

                def residual(b):
                    wait = waiter(dve, late)
                    wait("y_done", b + 1)
                    wait(f"stored{b}", 0)
                    at = late * TPG + 2 * b
                    x = X[:, slice(at, at + 2) if isinstance(late, int) else bass.ds(at, 2), :]
                    inc(dve.tensor_tensor(res[:, b, :, :], turned(banks[4 + b][:]), x, ALU.add), "res_done")

                if early is not None:
                    normalise()
                if late is not None:
                    scan(0)
                    scan(1)
                if early is not None:
                    xn_low(dve, early, 0)
                    convolve()
                    hidden(0)
                if late is not None:
                    memory_normed()
                if early is not None:
                    hidden(1)
                if late is not None:
                    memory_scaled(dve, late, 0)
                if early is not None:
                    hidden_low(dve, early, 0)
                if late is not None:
                    output_centered(0)
                if early is not None:
                    hidden(2)
                    norms()
                if late is not None:
                    output_centered(1)
                if early is not None:
                    hidden(3)
                if late is not None:
                    output_normed()
                if early is not None:
                    hidden(4)
                if late is not None:
                    gated(dve, late, 1)
                if early is not None:
                    hidden(5)
                    values(dve, early, 1)
                if late is not None:
                    output_low(0)
                    output_low(1)
                    residual(0)
                    residual(1)
                if early is not None:
                    mlp_added(0)
                    mlp_added(1)

            turns(dve, turn)

        @block.tensor
        def _(pe):
            def product(dst, lhs, rhs, last=True):
                n = 0
                for a, b in ((0, 0), (0, 1), (1, 0)):
                    for k in range(KC):
                        mm = pe.matmul(dst, lhs[a](k), rhs[b](k), start=(n == 0), stop=(last and n == 3 * KC - 1))
                        n += 1
                return mm

            def rows(hi, lo, t):
                return [lambda k, x=x: x[:, k, P * t:P * t + P] for x in (hi, lo)]

            def cols(a, b):
                return [lambda k, x=x: x[:, k, a:b] for x in (w_hi, w_lo)]

            def turn(late, early):
                def xn_turn(b):
                    wait = waiter(pe, early)
                    wait("xn_ready", 2 * b + 2)
                    wait("decay_done", 0)
                    for t in range(2 * b, 2 * b + 2):
                        for k in range(KC):
                            mm = pe.transpose(banks[b][:, SEQ * k + P * (t % 2):SEQ * k + P * (t % 2) + P], xn[:, t, k, :], ident[:])
                    inc(mm, "xn_turned")

                def query_key(t):
                    wait = waiter(pe, early)
                    wait("xn_hi_done", t // 2 + 1)
                    wait(f"xn_lo_done{t // 2}", 1)
                    if t >= 2:
                        wait("qk_sq", t - 1)
                    else:
                        wait("gates_done", 0)
                    inc(product(banks[2 + t % 2][:], rows(xn_hi, xn_lo, t), cols(W_QK, W_V)), "qk_done")

                def value(b):
                    wait = waiter(pe, early)
                    wait("xpad_done", b + 1)
                    for t in range(2 * b, 2 * b + 2):
                        mm = product(banks[b][:, D * (t % 2):D * (t % 2) + D], rows(xn_hi, xn_lo, t), cols(W_V, W_IO))
                    inc(mm, "v_done")

                def ffn_up(c):
                    wait = waiter(pe, early)
                    if c == 0:
                        wait("xn_hi_done", BPG)
                        wait("xn_lo_done0", 1)
                        wait("xn_lo_done1", 1)
                        wait("mlp_done", 0)
                    else:
                        wait("hid_done", c)
                    for bank, w in ((6, w1), (7, w2)):
                        n = 0
                        for x in (xn_hi, xn_lo):
                            for k in range(KC):
                                mm = pe.matmul(banks[bank][:], w[:, k, P * c:P * c + P], x[:, k, :], start=(n == 0), stop=(n == 3))
                                n += 1
                    inc(mm, "up_done")

                def ffn_down(b):
                    wait = waiter(pe, early)
                    if b == 0:
                        for c in range(FFN_CHUNKS):
                            wait(f"h_lo_done{c}", 1)
                        wait("hid_done", FFN_CHUNKS)
                    for t in range(2 * b, 2 * b + 2):
                        dst = banks[6 + b][:, D * (t % 2):D * (t % 2) + D]
                        for n, h in enumerate((h_hi, h_lo)):
                            for c in range(FFN_CHUNKS):
                                mm = pe.matmul(dst, h[:, c, P * t:P * t + P], w3[:, c, :], start=(n == 0 and c == 0), stop=(n == 1 and c == FFN_CHUNKS - 1))
                    inc(mm, "down_done")

                def gamma(m):
                    wait = waiter(pe, early)
                    wait("xc_lo_done", KC)
                    wait("vn_done", m + 1)
                    inc(product(banks[m][:], cols(W_G + P * m, W_G + P * m + P), [lambda k, x=x: x[:, k, :] for x in (xc_hi, xc_lo)]), "gamma_done")

                def gate(t):
                    wait = waiter(pe, early)
                    if t < 2:
                        wait("qk_sq", TPG)
                        wait("xc_lo_done", KC)
                    else:
                        wait("gates_done", t - 1)
                    bank = banks[2 + t % 2][:]
                    product(bank, rows(xc_hi, xc_lo, t), cols(W_IO, W_G), last=False)
                    inc(pe.matmul(bank, ones_rows[:], bias[:], start=False, stop=True), "io_done")

                def b_turn(b):
                    wait = waiter(pe, late)
                    wait(f"b_done{b}", 1)
                    wait("res_done", 0)
                    for t in range(2 * b, 2 * b + 2):
                        for m in range(KC):
                            mm = pe.transpose(banks[4 + b][:, SEQ * m + P * (t % 2):SEQ * m + P * (t % 2) + P], vn[:, t, P * m:P * m + P], ident[:])
                    inc(mm, "b_turned")

                def center_rows(b):
                    wait = waiter(pe, late)
                    wait("scan_done", b + 1)
                    for t in range(2 * b, 2 * b + 2):
                        for m in range(KC):
                            mm = pe.matmul(banks[4 + b][:, D * (t % 2) + P * m:D * (t % 2) + P * m + P], mem[:, m, P * t:P * t + P], center, start=True, stop=True)
                    inc(mm, "mem_centered")

                def o_turn(b):
                    wait = waiter(pe, late)
                    wait(f"o_done{b}", 1)
                    for t in range(2 * b, 2 * b + 2):
                        for m in range(KC):
                            mm = pe.transpose(banks[4 + b][:, SEQ * m + P * (t % 2):SEQ * m + P * (t % 2) + P], o[:, t, P * m:P * m + P], ident[:])
                    inc(mm, "o_turned")

                def output(b):
                    wait = waiter(pe, late)
                    wait("o_lo_done", b + 1)
                    for t in range(2):
                        mm = product(banks[4 + b][:, D * t:D * t + D], [lambda k, x=x: x[:, b, k, P * t:P * t + P] for x in (o_hi, o_lo)],
                                     [lambda k, x=x: x[:, k, :] for x in (wo_hi, wo_lo)])
                    inc(mm, "y_done")

                if late is not None:
                    b_turn(0)
                    b_turn(1)
                if early is not None:
                    xn_turn(0)
                    xn_turn(1)
                if late is not None:
                    center_rows(0)
                    center_rows(1)
                if early is not None:
                    query_key(0)
                    query_key(1)
                    ffn_up(0)
                    query_key(2)
                    value(0)
                    ffn_up(1)
                    value(1)
                    ffn_up(2)
                    query_key(3)
                    ffn_up(3)
                    gamma(0)
                    ffn_up(4)
                    gate(0)
                    gate(1)
                    ffn_up(5)
                    gamma(1)
                if late is not None:
                    o_turn(0)
                    o_turn(1)
                if early is not None:
                    gate(2)
                    gate(3)
                if late is not None:
                    output(0)
                    output(1)
                if early is not None:
                    ffn_down(0)
                    ffn_down(1)

            turns(pe, turn)


def build(nc, dram, out):
    with ExitStack() as stack:
        def sb(name, shape, dt=F32):
            return stack.enter_context(nc.sbuf_tensor(name, shape, dt))

        keep = {
            "X": sb("X", [P, TILES, D]),
            "ident": sb("ident", [P, P]),
            "eps": sb("eps", [P, 1]),
        }
        keep["shared"] = sb("shared", [P, KC * W_COLS])
        keep["rows"] = sb("rows", [P, PAIRS_N * WORDS // 2])
        keep["code_bytes"] = keep["rows"][:].bitcast(U16).rearrange("p (a n) -> p a n", n=WORDS)
        keep["stats"] = sb("stats", [P, TILES, 6])
        keep["raw_loaded"] = stack.enter_context(nc.semaphore("raw_loaded"))
        with (
            nc.sbuf_tensor("xall_hi", [P, KC, TOK], F32R) as keep["xall_hi"],
            nc.sbuf_tensor("xall_lo", [P, KC, TOK], F32R) as keep["xall_lo"],
        ):
            layer0_attention(nc, dram, keep)
            layer0_mlp(nc, dram, keep)
        layer1(nc, dram, keep, out)


def layouts(inputs, np):
    f = {k: np.asarray(v) for k, v in inputs.items()}
    a = {"x": f["L0_attn_x"].reshape(TOK, D)}

    def turned(w):
        return np.ascontiguousarray(w.T).reshape(P, KC, w.shape[0])

    wk = f["L0_attn_Wk"]
    a["wqkv"] = np.concatenate([turned(f["L0_attn_Wq"]), turned(wk), turned(wk), turned(f["L0_attn_Wv"])], axis=2)
    a["memory"] = f["L0_attn_memory"]
    a["memory_norm"] = f["L0_attn_memory_norm"]
    a["memory_weight"] = f["L0_attn_memory_weight"]
    c = np.zeros((P, NCONST), np.float32)
    c[:, C_ID:C_ID + P] = np.eye(P)
    for quad in range(2):
        for j in range(2):
            for hq in range(4):
                for d in range(DH):
                    src = 64 * j + (4 * quad + hq) * DH + d
                    v = 2 * (2 * quad + j)
                    for r, part in ((0, 0), (1, 1), (2, 0)):
                        c[src, C_SELQ + (v + part) * P + 3 * DH * hq + DH * r + d] = 1.0
    for h in range(HEADS):
        for d in range(DH):
            for r, part in ((0, 0), (1, 0), (2, 1)):
                c[64 * part + h * DH + d, C_SELK + h * P + 3 * DH * (h % 4) + DH * r + d] = 1.0
    c[64:, C_COL] = 1.0
    c[:64, C_COL + 1] = 1.0
    c[64:, C_COL + 1] = -1.0
    for hq in range(4):
        c[ROWS + 2 * hq:ROWS + 2 * hq + 2, C_COL + 2 + hq] = 1.0
    a["const"] = c

    def by_chunk(g):
        return g.reshape(PAIRS_N, P, 2, -1).transpose(3, 0, 2, 1).reshape(-1, PAIRS_N, D)

    gate, up = by_chunk(f["L0_ffn_gate_W_packed"]), by_chunk(f["L0_ffn_up_W_packed"])
    down = f["L0_ffn_down_W_packed"].T.reshape(PAIRS_N, P, D).transpose(1, 0, 2)
    a["codes"] = np.concatenate([gate, up, down], axis=2)
    rows = 2 * P // NVFP_BLOCK
    s_gate, s_up = by_chunk(f["L0_ffn_gate_scales"]), by_chunk(f["L0_ffn_up_scales"])
    s_down = f["L0_ffn_down_scales"].T.reshape(PAIRS_N, rows, D).transpose(1, 0, 2)
    a["scales"] = np.repeat(np.concatenate([s_gate, s_up, s_down], axis=2), P // rows, axis=0)

    l1 = {k[3:]: v for k, v in f.items() if k.startswith("L1_")}
    gamma_w = np.repeat(l1["attn_gamma_w"], L1_DH, axis=0)
    a["l1w"] = np.concatenate([turned(w) for w in (l1["attn_Wq"], l1["attn_Wk"], l1["attn_Wv"], l1["attn_ig_w"], l1["attn_og_w"], gamma_w)], axis=2)
    a["wo"] = l1["attn_Wo"].T.reshape(KC, P, D).transpose(1, 0, 2)
    a["conv"] = np.concatenate([l1["attn_conv_w"][:, 0, :].reshape(P, KC, TAPS), l1["attn_conv_b"].reshape(P, KC, 1)], axis=2)
    a["gamma_b"] = np.repeat(l1["attn_gamma_b"], L1_DH).reshape(KC, P).T
    a["scales_shifts"] = np.concatenate([l1["attn_" + n] for n in ("vn_g", "vn_b", "mn_g", "mn_b", "gn_g", "gn_b")]).reshape(1, -1)
    a["gate_bias"] = np.repeat(np.concatenate([l1["attn_ig_b"], l1["attn_og_b"]]).reshape(1, -1), 2, axis=0)
    wide = FFN_CHUNKS * P
    up = [np.concatenate([turned(l1[n]), np.zeros((P, KC, wide - FFN), np.float32)], axis=2).reshape(P, -1) for n in ("ffn_w1", "ffn_w2")]
    w3 = np.concatenate([l1["ffn_w3"].T, np.zeros((wide - FFN, D), np.float32)], axis=0)
    a["ternary"] = np.concatenate(up + [w3.reshape(FFN_CHUNKS, P, D).transpose(1, 0, 2).reshape(P, -1)], axis=1)
    c = np.zeros((P, N_CONST2), np.float32)
    c[0:2, C2_E:C2_E + P] = 1.0
    c[:, C2_CENTER:C2_CENTER + P] = np.eye(P) - np.kron(np.eye(P // L1_DH), np.full((L1_DH, L1_DH), 1.0 / L1_DH))
    c[1, C2_COL] = 1.0
    c[0, C2_COL + 1] = 1.0
    c[1, C2_COL + 1] = -1.0
    a["const2"] = c
    return a


def kernel(**inputs):
    import numpy as np
    import concourse.bacc as bacc
    from concourse.bass_utils import run_bass_kernel_spmd

    nc = bacc.Bacc("TRN2", target_bir_lowering=False, num_devices=1)
    arrays, dram = {}, {}
    for name, a in layouts(inputs, np).items():
        a = np.ascontiguousarray(a)
        arrays[f"in_{name}"] = a
        dram[name] = nc.dram_tensor(f"in_{name}", a.shape, mybir.dt.from_np(a.dtype), kind="ExternalInput").ap()
    out = nc.dram_tensor("out", (TOK, D), F32, kind="ExternalOutput").ap()
    build(nc, dram, out)
    r = run_bass_kernel_spmd(nc, [arrays], core_ids=[0])
    return r.results[0]["out"].reshape(BATCH, SEQ, D)
```
